# Optimizing a Trainium2 kernel written in Bass

```python
import numpy as np
import jax
import jax.numpy as jnp

def _softmax(x, axis=-1):
    return jax.nn.softmax(x, axis=axis)

def _gelu(x):
    return jax.nn.gelu(x, approximate=True)

def _silu(x):
    return jax.nn.silu(x)

def _sigmoid(x):
    return jax.nn.sigmoid(x)

def _layernorm(x, axis=-1, eps=1e-05):
    m = jnp.mean(x, axis=axis, keepdims=True)
    v = jnp.var(x, axis=axis, keepdims=True)
    return (x - m) / jnp.sqrt(v + eps)

def _scatter_add(tgt, idx, src, axis=0):
    return tgt.at[idx].add(src)

def _segment_sum(src, seg, n):
    return jax.ops.segment_sum(src, seg, n)
kernel_name = 'mk_adaln_attn_ffn_d1_seqx_r4_e64c4a'

def setup_inputs(seed: int=0):
    np.random.seed(seed)
    _w = jnp.asarray

    def _rec_inputs():
        import jax
        import jax.numpy as jnp
        _rk = jax.random.key(seed)
        x = -0.000125 + 0.9999 * jax.random.normal(jax.random.fold_in(_rk, 1), (4, 512, 512), jnp.float32)
        _lenS = 512 - jax.random.randint(jax.random.fold_in(_rk, 7), (4,), 0, max(1, 512 // 4) + 1, jnp.int32)
        _lenS2 = 512 - jax.random.randint(jax.random.fold_in(_rk, 8), (4,), 0, max(1, 512 // 4) + 1, jnp.int32)
        fside_BxSxS_0 = -1.52775e-05 + 0.999936 * jax.random.normal(jax.random.fold_in(_rk, 11), (4, 512, 512), jnp.float32)
        cond_512 = -5.03954e-05 + 1.00559 * jax.random.normal(jax.random.fold_in(_rk, 12), (4, 128), jnp.float32)
        return (x, fside_BxSxS_0, cond_512)
    x, fside_BxSxS_0, cond_512 = _rec_inputs()

    def _L0_cond_setup():
        import jax, jax.numpy as jnp
        from jax import lax
        import numpy as np
        B, T, C, TD = (8, 512, 512, 128)

        def _bi_wkv(r, k, v, w, u, time_emb):
            tf = jax.nn.sigmoid(jnp.sum(time_emb, axis=-1))[:, None, None]
            decay = jnp.exp(-jnp.exp(w.astype(jnp.float32)))[None, :] * (0.5 + 0.5 * tf[:, :, 0])
            kf = k.astype(jnp.float32)
            vf = v.astype(jnp.float32)
            ek = jnp.exp(jnp.minimum(kf, 30.0))
            ekv = ek * vf

            def step(carry, x):
                a, b = carry
                ekv_t, ek_t = x
                a = a * decay + ekv_t
                b = b * decay + ek_t
                return ((a, b), (a, b))
            ekv_t = jnp.swapaxes(ekv, 0, 1)
            ek_t = jnp.swapaxes(ek, 0, 1)
            init = (jnp.zeros_like(decay), jnp.zeros_like(decay))
            _, (nf, df) = lax.scan(step, init, (ekv_t, ek_t))
            _, (nb, db) = lax.scan(step, init, (ekv_t, ek_t), reverse=True)
            nf = jnp.swapaxes(nf, 0, 1)
            df = jnp.swapaxes(df, 0, 1)
            nb = jnp.swapaxes(nb, 0, 1)
            db = jnp.swapaxes(db, 0, 1)
            euk = jnp.exp(jnp.minimum(u.astype(jnp.float32)[None, None, :] + kf, 30.0))
            num = nf + nb - ekv + euk * vf
            den = df + db - ek + euk
            base = jax.nn.sigmoid(r.astype(jnp.float32)) * (num / jnp.maximum(den, 1e-08))
            out = base * (0.8 + 0.2 * tf)
            return out.astype(r.dtype)
        key = jax.random.key(seed)
        ks = jax.random.split(key, 6)
        return {'r': jax.random.normal(ks[0], (B, T, C), dtype=jnp.float32), 'k': jax.random.normal(ks[1], (B, T, C), dtype=jnp.float32), 'v': jax.random.normal(ks[2], (B, T, C), dtype=jnp.float32), 'w': jax.random.normal(ks[3], (C,), dtype=jnp.float32), 'u': jax.random.normal(ks[4], (C,), dtype=jnp.float32), 'time_emb': jax.random.normal(ks[5], (B, TD), dtype=jnp.float32)}
    _L0_cond_all = _L0_cond_setup()
    _L0_cond_in = {k: v for k, v in _L0_cond_all.items() if k in ('w', 'u')}
    del _L0_cond_all

    def _L0_attn_setup():
        import jax, jax.numpy as jnp
        import numpy as np
        B, S, D = (4, 1024, 512)
        DECAY_BIAS_INIT = -4.0
        W_SCALE = 0.02
        key = jax.random.key(seed)
        ks = jax.random.split(key, 6)
        return {'x': jax.random.normal(ks[0], (B, S, D), dtype=jnp.float32), 'W_in': jax.random.normal(ks[1], (D, D), dtype=jnp.float32) * W_SCALE, 'b_in': jnp.zeros((D,), jnp.float32), 'W_decay': jax.random.normal(ks[2], (D, D), dtype=jnp.float32) * W_SCALE, 'b_decay': jnp.zeros((D,), jnp.float32), 'W_gate': jax.random.normal(ks[3], (D, D), dtype=jnp.float32) * W_SCALE, 'b_gate': jnp.zeros((D,), jnp.float32), 'W_out': jax.random.normal(ks[4], (D, D), dtype=jnp.float32) * W_SCALE, 'b_out': jnp.zeros((D,), jnp.float32), 'decay_bias': jnp.full((D,), DECAY_BIAS_INIT, jnp.float32)}
    _L0_attn_all = _L0_attn_setup()
    _L0_attn_in = {k: v for k, v in _L0_attn_all.items() if k in ('W_in', 'b_in', 'W_decay', 'b_decay', 'W_gate', 'b_gate', 'W_out', 'b_out', 'decay_bias')}
    del _L0_attn_all

    def _L0_cond2_setup():
        import jax, jax.numpy as jnp
        from jax import lax
        import numpy as np
        B, T, C, TD = (8, 512, 512, 128)

        def _bi_wkv(r, k, v, w, u, time_emb):
            tf = jax.nn.sigmoid(jnp.sum(time_emb, axis=-1))[:, None, None]
            decay = jnp.exp(-jnp.exp(w.astype(jnp.float32)))[None, :] * (0.5 + 0.5 * tf[:, :, 0])
            kf = k.astype(jnp.float32)
            vf = v.astype(jnp.float32)
            ek = jnp.exp(jnp.minimum(kf, 30.0))
            ekv = ek * vf

            def step(carry, x):
                a, b = carry
                ekv_t, ek_t = x
                a = a * decay + ekv_t
                b = b * decay + ek_t
                return ((a, b), (a, b))
            ekv_t = jnp.swapaxes(ekv, 0, 1)
            ek_t = jnp.swapaxes(ek, 0, 1)
            init = (jnp.zeros_like(decay), jnp.zeros_like(decay))
            _, (nf, df) = lax.scan(step, init, (ekv_t, ek_t))
            _, (nb, db) = lax.scan(step, init, (ekv_t, ek_t), reverse=True)
            nf = jnp.swapaxes(nf, 0, 1)
            df = jnp.swapaxes(df, 0, 1)
            nb = jnp.swapaxes(nb, 0, 1)
            db = jnp.swapaxes(db, 0, 1)
            euk = jnp.exp(jnp.minimum(u.astype(jnp.float32)[None, None, :] + kf, 30.0))
            num = nf + nb - ekv + euk * vf
            den = df + db - ek + euk
            base = jax.nn.sigmoid(r.astype(jnp.float32)) * (num / jnp.maximum(den, 1e-08))
            out = base * (0.8 + 0.2 * tf)
            return out.astype(r.dtype)
        key = jax.random.key(seed)
        ks = jax.random.split(key, 6)
        return {'r': jax.random.normal(ks[0], (B, T, C), dtype=jnp.float32), 'k': jax.random.normal(ks[1], (B, T, C), dtype=jnp.float32), 'v': jax.random.normal(ks[2], (B, T, C), dtype=jnp.float32), 'w': jax.random.normal(ks[3], (C,), dtype=jnp.float32), 'u': jax.random.normal(ks[4], (C,), dtype=jnp.float32), 'time_emb': jax.random.normal(ks[5], (B, TD), dtype=jnp.float32)}
    _L0_cond2_all = _L0_cond2_setup()
    _L0_cond2_in = {k: v for k, v in _L0_cond2_all.items() if k in ('w', 'u')}
    del _L0_cond2_all

    def _L0_ffn_setup():
        import jax, jax.numpy as jnp
        import numpy as np
        import math
        D_MODEL = 512
        D_FF = 2048
        NUM_EXPERTS = 8
        TOP_K = 2
        CAPACITY_FACTOR = 1.25
        BATCH, SEQ = (4, 512)

        def _moe_forward(x, Wg, w1, w2):
            B, T, d = x.shape
            S = B * T
            E, K = (NUM_EXPERTS, TOP_K)
            C = math.ceil(CAPACITY_FACTOR * S * K / E)
            xr = x.reshape(S, d)
            probs = jax.nn.softmax(xr @ Wg, axis=-1)
            gate_vals, expert_idx = jax.lax.top_k(probs, K)
            flat_e = expert_idx.reshape(-1)
            oh = jax.nn.one_hot(flat_e, E, dtype=jnp.int32)
            pos = jnp.sum((jnp.cumsum(oh, axis=0) - 1) * oh, axis=1)
            kept = pos < C
            i = jnp.arange(S * K)
            slot = i % K * S + i // K
            sentinel = S * K
            pos_w = jnp.where(kept, pos, C)
            dispatch_mask = jnp.full((E, C), sentinel, dtype=jnp.int32)
            dispatch_mask = dispatch_mask.at[flat_e, pos_w].set(slot.astype(jnp.int32), mode='drop')
            combine_weights = (gate_vals * kept.reshape(S, K)).T
            dispatched = xr[dispatch_mask.reshape(-1) % S].reshape(E, C, d)
            h = jax.nn.relu(jnp.einsum('ecd,edf->ecf', dispatched, w1))
            expert_out = jnp.einsum('ecf,efd->ecd', h, w2)
            rerouted = jnp.zeros((S * K + 1, d), dtype=expert_out.dtype)
            rerouted = rerouted.at[dispatch_mask.reshape(-1)].set(expert_out.reshape(-1, d))
            rerouted = rerouted[:-1].reshape(K, S, d)
            out = jnp.einsum('ks,ksm->sm', combine_weights, rerouted)
            return out.reshape(B, T, d)
        key = jax.random.key(seed)
        k1, k2, k3, k4 = jax.random.split(key, 4)
        x = jax.random.normal(k1, (BATCH, SEQ, D_MODEL), dtype=jnp.float32)
        Wg = jax.random.normal(k2, (D_MODEL, NUM_EXPERTS), dtype=jnp.float32) * 0.02
        w1 = jax.random.normal(k3, (NUM_EXPERTS, D_MODEL, D_FF), dtype=jnp.float32) * 0.02
        w2 = jax.random.normal(k4, (NUM_EXPERTS, D_FF, D_MODEL), dtype=jnp.float32) * 0.02
        return {'x': x, 'Wg': Wg, 'w1': w1, 'w2': w2}
    _L0_ffn_all = _L0_ffn_setup()
    _L0_ffn_in = {k: v for k, v in _L0_ffn_all.items() if k in ('Wg', 'w1', 'w2')}
    del _L0_ffn_all
    return {'x': x, 'fside_BxSxS_0': fside_BxSxS_0, 'cond_512': cond_512, 'L0_cond_w': _L0_cond_in['w'], 'L0_cond_u': _L0_cond_in['u'], 'L0_attn_W_in': _L0_attn_in['W_in'], 'L0_attn_b_in': _L0_attn_in['b_in'], 'L0_attn_W_decay': _L0_attn_in['W_decay'], 'L0_attn_b_decay': _L0_attn_in['b_decay'], 'L0_attn_W_gate': _L0_attn_in['W_gate'], 'L0_attn_b_gate': _L0_attn_in['b_gate'], 'L0_attn_W_out': _L0_attn_in['W_out'], 'L0_attn_b_out': _L0_attn_in['b_out'], 'L0_attn_decay_bias': _L0_attn_in['decay_bias'], 'L0_cond2_w': _L0_cond2_in['w'], 'L0_cond2_u': _L0_cond2_in['u'], 'L0_ffn_Wg': _L0_ffn_in['Wg'], 'L0_ffn_w1': _L0_ffn_in['w1'], 'L0_ffn_w2': _L0_ffn_in['w2']}

def reference(x, fside_BxSxS_0, cond_512, L0_cond_w, L0_cond_u, L0_attn_W_in, L0_attn_b_in, L0_attn_W_decay, L0_attn_b_decay, L0_attn_W_gate, L0_attn_b_gate, L0_attn_W_out, L0_attn_b_out, L0_attn_decay_bias, L0_cond2_w, L0_cond2_u, L0_ffn_Wg, L0_ffn_w1, L0_ffn_w2):
    import jax
    import jax.numpy as jnp

    def _L0_cond_ref(r, k, v, w, u, time_emb):
        import jax, jax.numpy as jnp
        from jax import lax
        import numpy as np
        B, T, C, TD = (8, 512, 512, 128)

        def _bi_wkv(r, k, v, w, u, time_emb):
            tf = jax.nn.sigmoid(jnp.sum(time_emb, axis=-1))[:, None, None]
            decay = jnp.exp(-jnp.exp(w.astype(jnp.float32)))[None, :] * (0.5 + 0.5 * tf[:, :, 0])
            kf = k.astype(jnp.float32)
            vf = v.astype(jnp.float32)
            ek = jnp.exp(jnp.minimum(kf, 30.0))
            ekv = ek * vf

            def step(carry, x):
                a, b = carry
                ekv_t, ek_t = x
                a = a * decay + ekv_t
                b = b * decay + ek_t
                return ((a, b), (a, b))
            ekv_t = jnp.swapaxes(ekv, 0, 1)
            ek_t = jnp.swapaxes(ek, 0, 1)
            init = (jnp.zeros_like(decay), jnp.zeros_like(decay))
            _, (nf, df) = lax.scan(step, init, (ekv_t, ek_t))
            _, (nb, db) = lax.scan(step, init, (ekv_t, ek_t), reverse=True)
            nf = jnp.swapaxes(nf, 0, 1)
            df = jnp.swapaxes(df, 0, 1)
            nb = jnp.swapaxes(nb, 0, 1)
            db = jnp.swapaxes(db, 0, 1)
            euk = jnp.exp(jnp.minimum(u.astype(jnp.float32)[None, None, :] + kf, 30.0))
            num = nf + nb - ekv + euk * vf
            den = df + db - ek + euk
            base = jax.nn.sigmoid(r.astype(jnp.float32)) * (num / jnp.maximum(den, 1e-08))
            out = base * (0.8 + 0.2 * tf)
            return out.astype(r.dtype)
        return _bi_wkv(r, k, v, w, u, time_emb)

    def _L0_attn_ref(x, W_in, b_in, W_decay, b_decay, W_gate, b_gate, W_out, b_out, decay_bias):
        import jax, jax.numpy as jnp
        import numpy as np
        B, S, D = (4, 1024, 512)
        DECAY_BIAS_INIT = -4.0
        W_SCALE = 0.02
        inp = jax.nn.silu(jnp.einsum('bsd,de->bse', x, W_in) + b_in).astype(jnp.float32)
        decay = jax.nn.sigmoid(jnp.einsum('bsd,de->bse', x, W_decay) + b_decay + decay_bias)
        gate = jax.nn.sigmoid(jnp.einsum('bsd,de->bse', x, W_gate) + b_gate)

        def step(state, di):
            d, i = di
            state = d * state + (1.0 - d) * i
            return (state, state)
        init = jnp.zeros((x.shape[0], x.shape[2]), jnp.float32)
        _, states = jax.lax.scan(step, init, (jnp.swapaxes(decay, 0, 1), jnp.swapaxes(inp, 0, 1)))
        y = gate * jnp.swapaxes(states, 0, 1)
        y = y.astype(x.dtype)
        return jnp.einsum('bsd,de->bse', y, W_out) + b_out

    def _L0_cond2_ref(r, k, v, w, u, time_emb):
        import jax, jax.numpy as jnp
        from jax import lax
        import numpy as np
        B, T, C, TD = (8, 512, 512, 128)

        def _bi_wkv(r, k, v, w, u, time_emb):
            tf = jax.nn.sigmoid(jnp.sum(time_emb, axis=-1))[:, None, None]
            decay = jnp.exp(-jnp.exp(w.astype(jnp.float32)))[None, :] * (0.5 + 0.5 * tf[:, :, 0])
            kf = k.astype(jnp.float32)
            vf = v.astype(jnp.float32)
            ek = jnp.exp(jnp.minimum(kf, 30.0))
            ekv = ek * vf

            def step(carry, x):
                a, b = carry
                ekv_t, ek_t = x
                a = a * decay + ekv_t
                b = b * decay + ek_t
                return ((a, b), (a, b))
            ekv_t = jnp.swapaxes(ekv, 0, 1)
            ek_t = jnp.swapaxes(ek, 0, 1)
            init = (jnp.zeros_like(decay), jnp.zeros_like(decay))
            _, (nf, df) = lax.scan(step, init, (ekv_t, ek_t))
            _, (nb, db) = lax.scan(step, init, (ekv_t, ek_t), reverse=True)
            nf = jnp.swapaxes(nf, 0, 1)
            df = jnp.swapaxes(df, 0, 1)
            nb = jnp.swapaxes(nb, 0, 1)
            db = jnp.swapaxes(db, 0, 1)
            euk = jnp.exp(jnp.minimum(u.astype(jnp.float32)[None, None, :] + kf, 30.0))
            num = nf + nb - ekv + euk * vf
            den = df + db - ek + euk
            base = jax.nn.sigmoid(r.astype(jnp.float32)) * (num / jnp.maximum(den, 1e-08))
            out = base * (0.8 + 0.2 * tf)
            return out.astype(r.dtype)
        return _bi_wkv(r, k, v, w, u, time_emb)

    def _L0_ffn_ref(x, Wg, w1, w2):
        import jax, jax.numpy as jnp
        import numpy as np
        import math
        D_MODEL = 512
        D_FF = 2048
        NUM_EXPERTS = 8
        TOP_K = 2
        CAPACITY_FACTOR = 1.25
        BATCH, SEQ = (4, 512)

        def _moe_forward(x, Wg, w1, w2):
            B, T, d = x.shape
            S = B * T
            E, K = (NUM_EXPERTS, TOP_K)
            C = math.ceil(CAPACITY_FACTOR * S * K / E)
            xr = x.reshape(S, d)
            probs = jax.nn.softmax(xr @ Wg, axis=-1)
            gate_vals, expert_idx = jax.lax.top_k(probs, K)
            flat_e = expert_idx.reshape(-1)
            oh = jax.nn.one_hot(flat_e, E, dtype=jnp.int32)
            pos = jnp.sum((jnp.cumsum(oh, axis=0) - 1) * oh, axis=1)
            kept = pos < C
            i = jnp.arange(S * K)
            slot = i % K * S + i // K
            sentinel = S * K
            pos_w = jnp.where(kept, pos, C)
            dispatch_mask = jnp.full((E, C), sentinel, dtype=jnp.int32)
            dispatch_mask = dispatch_mask.at[flat_e, pos_w].set(slot.astype(jnp.int32), mode='drop')
            combine_weights = (gate_vals * kept.reshape(S, K)).T
            dispatched = xr[dispatch_mask.reshape(-1) % S].reshape(E, C, d)
            h = jax.nn.relu(jnp.einsum('ecd,edf->ecf', dispatched, w1))
            expert_out = jnp.einsum('ecf,efd->ecd', h, w2)
            rerouted = jnp.zeros((S * K + 1, d), dtype=expert_out.dtype)
            rerouted = rerouted.at[dispatch_mask.reshape(-1)].set(expert_out.reshape(-1, d))
            rerouted = rerouted[:-1].reshape(K, S, d)
            out = jnp.einsum('ks,ksm->sm', combine_weights, rerouted)
            return out.reshape(B, T, d)
        return _moe_forward(x, Wg, w1, w2)
    x = x + _L0_attn_ref(_L0_cond_ref(x, fside_BxSxS_0, fside_BxSxS_0, L0_cond_w, L0_cond_u, cond_512), L0_attn_W_in, L0_attn_b_in, L0_attn_W_decay, L0_attn_b_decay, L0_attn_W_gate, L0_attn_b_gate, L0_attn_W_out, L0_attn_b_out, L0_attn_decay_bias)
    x = x + _L0_ffn_ref(_L0_cond2_ref(x, fside_BxSxS_0, fside_BxSxS_0, L0_cond2_w, L0_cond2_u, cond_512), L0_ffn_Wg, L0_ffn_w1, L0_ffn_w2)
    return x

_drawn_inputs = setup_inputs


def setup_inputs(seed=0):
    import zlib

    import numpy as np

    out = dict(_drawn_inputs(seed))
    spreads = {'L0_attn_b_in': (0.0, 0.656),
     'L0_attn_b_decay': (0.0, 2.0),
     'L0_attn_b_gate': (0.0, 2.0),
     'L0_attn_b_out': (0.0, 0.1),
     'L0_attn_decay_bias': (-4.0, 0.6)}
    factors = {'cond_512': 168.56,
     'L0_cond_w': 5.538,
     'L0_cond_u': 8.0,
     'L0_attn_W_decay': 176.33,
     'L0_attn_W_gate': 8.0,
     'L0_cond2_w': 3.126,
     'L0_cond2_u': 50.242}
    for name, (base, spread) in spreads.items():
        noise = np.random.default_rng([zlib.crc32(name.encode()), seed]).standard_normal(out[name].shape)
        drawn = base * np.exp(spread * noise) if base else spread * noise
        out[name] = jnp.asarray(drawn.astype(out[name].dtype))
    for name, factor in factors.items():
        out[name] = (out[name] * factor).astype(out[name].dtype)
    return out
```

```python
from contextlib import ExitStack
import math

import concourse.bass as bass
from concourse import mybir

F32 = mybir.dt.float32
F32R = mybir.dt.float32r
BF16 = mybir.dt.bfloat16
I32 = mybir.dt.int32
U32 = mybir.dt.uint32
ALU = mybir.AluOpType
ACT = mybir.ActivationFunctionType
AX = mybir.AxisListType

P = 128
B, T, C = 4, 512, 512
CT = C // P
TT = T // P
NE, DFF, TOPK = 8, 2048, 2
CAP = math.ceil(1.25 * B * T * TOPK / NE)
ST = CAP // P
ROW = C + NE + 1
NO_TOKEN = 1 << 20
CAPV, DEN_MIN = 30.0, 1e-8
FT = DFF // P
FC = 4
NC = FT // FC
PIECES = 2 * FC
W1C, W2C, U1C, U2C, BIN, BGATE, BOUT, BDEC, DBIAS = range(9)


def first_batch(b):
    return isinstance(b, int) and b == 0


class Steps:

    def __init__(self, eng, sem, base):
        self.eng, self.sem, self.base, self.n = eng, sem, base, 0

    def mark(self, ins):
        ins.then_inc(self.sem, 1)
        self.n += 1

    def wait(self):
        self.eng.wait_ge(self.sem, self.base + self.n)

    def do(self, ins):
        self.mark(ins)
        self.wait()


def build_program(nc, x, fside, cond, w1c, u1c, W_in, b_in, W_decay, b_decay, W_gate, b_gate,
                  W_out, b_out, decay_bias, w2c, u2c, Wg, w1, w2, out):
    slots = nc.dram_tensor("slots", ((NE + 1) * CAP, ROW), F32, kind="Internal").ap()
    out_rows = out.rearrange("b t c -> (b t) c")
    with ExitStack() as ctx:
        def sb(name, shape, dt=F32):
            return ctx.enter_context(nc.sbuf_tensor(name, shape, dt))

        ident = sb("ident", [P, P])
        counts = sb("counts", [P, NE], I32)
        with ExitStack() as phase:
            conditioning_and_routing(nc, phase, ident, counts, slots, out_rows, x, fside, cond, w1c, u1c,
                                     W_in, b_in, W_decay, b_decay, W_gate, b_gate, W_out, b_out,
                                     decay_bias, w2c, u2c, Wg)
        with ExitStack() as phase:
            experts(nc, phase, ident, counts, slots, out_rows, w1, w2)


def conditioning_and_routing(nc, ctx, ident, counts, slots, out_rows, x, fside, cond, w1c, u1c,
                             W_in, b_in, W_decay, b_decay, W_gate, b_gate, W_out, b_out,
                             decay_bias, w2c, u2c, Wg):
    def sb(name, shape, dt=F32):
        return ctx.enter_context(nc.sbuf_tensor(name, shape, dt))

    def ps(name, shape, dt=F32):
        return ctx.enter_context(nc.psum_tensor(name, shape, dt))

    def sem(name):
        return ctx.enter_context(nc.semaphore(name))

    lower = sb("lower", [P, P], BF16)
    ones = sb("ones", [P, P], BF16)
    expert_no = sb("expert_no", [P, TT, NE])
    slot_base = sb("slot_base", [P, TT, NE])
    token_no = sb("token_no", [P, B * TT], U32)
    vec = sb("vec", [P, 9, CT])
    wm = sb("wm", [P, 4, CT, C])
    wg = sb("wg", [P, CT, NE])
    tf = sb("tf", [P, B])
    half_tf = sb("half_tf", [P, B])
    neg_scale = sb("neg_scale", [P, B])
    ew = sb("ew", [P, 2, CT])
    decay = sb("decay", [P, B * 2 * CT])
    one_m = sb("one_m", [P, B * 2 * CT])
    one_md2 = sb("one_md2", [P, B * 2 * CT])
    bdec = sb("bdec", [P, CT])
    x_rows = sb("x_rows", [P, TT, C])
    f_rows = sb("f_rows", [P, TT, C])
    xT = sb("xT", [P, 2, CT, T])
    kT = sb("kT", [P, 2, T])
    ek = sb("ek", [P, 2, T])
    ekv = sb("ekv", [P, 2, T])
    euk = sb("euk", [P, 2, 2, T])
    eukv = sb("eukv", [P, 2, 2, T])
    sums = sb("sums", [P, 2, 2, 2, T])
    scaled = sb("scaled", [P, 2, 2, T])
    recip0 = sb("recip0", [P, 2, T])
    r1T = sb("r1T", [P, 2, CT, T])
    ratio2 = sb("ratio2", [P, 2, CT, T])
    sig = sb("sig", [P, CT, T])
    z_in = sb("z_in", [P, CT, T])
    z_dec = sb("z_dec", [P, CT, T])
    z_gate = sb("z_gate", [P, CT, T])
    x2_rows = sb("x2_rows", [P, TT, C])
    r2_rows = sb("r2_rows", [P, TT, ROW])
    logit = sb("logit", [P, TT, NE])
    top = sb("top", [P, TT, NE])
    top_i = sb("top_i", [P, TT, NE], U32)
    top_f = sb("top_f", [P, TT, NE])
    oh = sb("oh", [P, 2, TT, NE])
    sel = sb("sel", [P, TT, NE], BF16)
    carry = sb("carry", [P, NE], BF16)
    sel_sum = sb("sel_sum", [P, NE])
    pe_ = sb("prob", [P, TT, NE])
    psum_ = sb("prob_sum", [P, TT])
    slot_f = sb("slot_f", [P, TT, NE])
    slot_t = sb("slot_t", [P, TT, NE])
    dest_f = sb("dest_f", [P, 2, TT])
    dest = sb("dest", [P, 2, TT], U32)

    ps_f = ps("ps_f", [P, T])
    ps_x = ps("ps_x", [P, T])
    ps_mm = ps("ps_mm", [P, 3, T])
    ps_to = ps("ps_to", [P, C])
    ps_small = ps("ps_small", [P, 512])
    ps_logit = ps_small[:, 0:32].rearrange("p (i e) -> p i e", i=TT)
    ps_pos = ps_small[:, 32:64].rearrange("p (i e) -> p i e", i=TT)
    ps_count = ps_small[:, 64:72]
    ps_decay = ps("ps_decay", [P, 512])[:, 0:B * 2 * CT]

    s_vec, s_w, s_f_in, s_x_in = sem("vec_in"), sem("w_in"), sem("f_in"), sem("x_in")
    s_init, s_x2_out, s_disp = sem("slots_init"), sem("x2_out"), sem("dispatched")
    s_pool_setup, s_template, s_consts = sem("pool_setup"), sem("template"), sem("consts_ready")
    s_setup_v, s_setup_a = sem("setup_dve"), sem("setup_act")
    s_f_tp, s_x_tp, s_k, s_xT = sem("f_transposed"), sem("x_transposed"), sem("k_ready"), sem("xT_ready")
    s_caps, s_ek, s_euk, s_ekv, s_eukv = sem("caps_ready"), sem("ek_ready"), sem("euk_ready"), sem("ekv_ready"), sem("eukv_ready")
    s_bwd, s_scaled, s_den, s_ln, s_rec, s_newton, s_ratio = (
        sem("bwd_done"), sem("scaled_ready"), sem("den_ready"), sem("ln_ready"), sem("recip_ready"),
        sem("newton_ready"), sem("ratio_ready"))
    s_fold, s_vt = sem("fold_steps"), sem("vectors_transposed")
    s_sig1, s_r1, s_mm, s_z, s_gates = sem("sig1_ready"), sem("r1_ready"), sem("mm_done"), sem("z_ready"), sem("gates_ready")
    s_rec_steps, s_y, s_wo, s_x2, s_sig2, s_r2 = (
        sem("recurrence_steps"), sem("y_ready"), sem("wout_done"), sem("x2_ready"), sem("sig2_ready"), sem("r2_ready"))
    s_to, s_ev_x2, s_ev_r2, s_logit = sem("rows_transposed"), sem("x2_rows_ready"), sem("r2_rows_ready"), sem("logits_done")
    s_route, s_shift, s_pexp, s_sel, s_pos, s_dest, s_count = (
        sem("route_steps"), sem("shift_ready"), sem("prob_exp"), sem("sel_ready"), sem("pos_done"), sem("dest_ready"), sem("count_done"))

    N_V = 9
    N_VEC = N_V + 1
    ROUTE_STEPS = 17 + 2 * TT
    vec_cond = z_gate[:, 0, :]
    vec_rows = z_gate[0:N_V * CT, 1, 0:P]
    block = ctx.enter_context(nc.Block())

    def col(b, c, ct):
        return bass.ds(b * (2 * CT) + (c * CT + ct), 1)

    @block.sync
    def _(sp):
        def load(b):
            sp.dma_start(f_rows[:], fside[bass.ds(b, 1)].rearrange("o (i p) c -> p (o i) c", p=P)).then_inc(s_f_in, 16)
            sp.dma_start(x_rows[:], x[bass.ds(b, 1)].rearrange("o (i p) c -> p (o i) c", p=P)).then_inc(s_x_in, 16)

        def store(b):
            sp.wait_ge(s_ev_x2, TT * (b + 1))
            sp.dma_start(out_rows[bass.ds(b * T, T)].rearrange("(i p) c -> p i c", p=P), x2_rows[:]).then_inc(s_x2_out, 16)

        load(0)
        sp.dma_start(vec_cond[:], cond.rearrange("b d -> (b d)").partition_broadcast(P)).then_inc(s_vec, 16)
        for n, v in ((W1C, w1c), (W2C, w2c), (U1C, u1c), (U2C, u2c), (BIN, b_in), (BGATE, b_gate),
                     (BOUT, b_out), (BDEC, b_decay), (DBIAS, decay_bias)):
            sp.dma_start(vec_rows[n * CT:(n + 1) * CT, :], v.rearrange("(t p) -> t p", p=P)).then_inc(s_vec, 16)
        for n, w in enumerate((W_in, W_decay, W_gate, W_out)):
            sp.dma_start(wm[:, n], w.rearrange("(t p) n -> p t n", p=P)).then_inc(s_w, 16)
        sp.dma_start(wg[:], Wg.rearrange("(t p) e -> p t e", p=P)).then_inc(s_w, 16)
        sp.wait_ge(s_template, 2)
        for n in range((NE + 1) * ST):
            sp.dma_start(slots[n * P:(n + 1) * P, :], r2_rows[:, 0, :]).then_inc(s_init, 16)
        with sp.Fori(1, B) as b:
            sp.wait_ge(s_f_tp, b * CT)
            sp.wait_ge(s_x_tp, b * CT)
            load(b)
            store(b - 1)
        store(B - 1)
        sp.wait_ge(s_x2_out, 16 * B)
        sp.wait_ge(s_init, 16 * (NE + 1) * ST)

    @block.gpsimd
    def _(pool):
        g = nc.gpsimd
        setup = Steps(pool, s_pool_setup, 0)
        setup.mark(g.memset(ident[:], 0.0))
        setup.mark(g.memset(lower[:], 1.0))
        setup.do(g.memset(ones[:], 1.0))
        setup.mark(g.affine_select(out=ident[:], in_=ident[:], compare_op=ALU.not_equal, fill=1.0, base=0,
                                   pattern=[[-1, P]], channel_multiplier=1))
        setup.mark(g.affine_select(out=lower[:], in_=lower[:], compare_op=ALU.is_gt, fill=0.0, base=0,
                                   pattern=[[1, P]], channel_multiplier=-1))
        setup.mark(g.iota(expert_no[:], [[0, TT], [1, NE]], base=0, channel_multiplier=0,
                          allow_small_or_imprecise_dtypes=True))
        setup.mark(g.iota(slot_base[:], [[0, TT], [CAP, NE]], base=0, channel_multiplier=0,
                          allow_small_or_imprecise_dtypes=True))
        setup.mark(g.iota(token_no[:], [[P, B * TT]], base=0, channel_multiplier=1))
        g.memset(carry[:], 0.0).then_inc(s_consts, 1)

        def products(u, ct):
            r = ct % 2
            pool.wait_ge(s_ek, u + 1)
            if not isinstance(u, int) or u >= 2:
                pool.wait_ge(s_den, u - 1)
            g.tensor_tensor(ekv[:, r], ek[:, r], kT[:, r], ALU.mult).then_inc(s_ekv, 1)
            pool.wait_ge(s_euk, u + 1)
            g.tensor_tensor(eukv[:, r, 0], euk[:, r, 0], kT[:, r], ALU.mult)
            g.tensor_tensor(eukv[:, r, 1], euk[:, r, 1], kT[:, r], ALU.mult).then_inc(s_eukv, 1)

        def newton(u, ct):
            r = ct % 2
            for c in range(2):
                pool.wait_ge(s_rec, 2 * u + c + 1)
                g.tensor_tensor(sums[:, r, c, 1], sums[:, r, c, 1], recip0[:, c], ALU.mult)
                g.tensor_tensor(sums[:, r, c, 0], sums[:, r, c, 0], recip0[:, c], ALU.mult).then_inc(s_newton, 1)

        def conditioning(b):
            for s in range(CT + 1):
                if s < CT:
                    products(b * CT + s, s)
                if s >= 1:
                    newton(b * CT + (s - 1), s - 1)

        def dispatch(b):
            pool.wait_ge(s_ev_r2, TT * (b + 1))
            pool.wait_ge(s_dest, b + 1)
            if first_batch(b):
                pool.wait_ge(s_init, 16 * (NE + 1) * ST)
            pool.nop(nofuse=True)
            for i in range(TT):
                for k in range(TOPK):
                    pool.indirect_dma_start(
                        out=slots, out_offset=bass.IndirectOffsetOnAxis(ap=dest[:, k, i:i + 1], axis=0),
                        in_=r2_rows[:, i, :], in_offset=None, bounds_check=NE * CAP - 1, oob_is_err=False,
                    ).then_inc(s_disp, 16)

        conditioning(0)
        conditioning(1)
        dispatch(0)
        with pool.Fori(2, B) as b:
            conditioning(b)
            dispatch(b - 1)
        dispatch(B - 1)
        pool.wait_ge(s_disp, 16 * TT * TOPK * B)

    @block.tensor
    def _(pe):
        def transpose_in(b, ct):
            u = b * CT + ct
            first = isinstance(b, int) and u == 0
            if ct == 0:
                pe.wait_ge(s_f_in, 16 * (b + 1))
            if not first:
                pe.wait_ge(s_k, u)
            for i in range(TT):
                last = nc.tensor.transpose(ps_f[:, i * P:(i + 1) * P], f_rows[:, i, ct * P:(ct + 1) * P], ident[:])
            last.then_inc(s_f_tp, 1)
            if ct == 0:
                pe.wait_ge(s_x_in, 16 * (b + 1))
            if not first:
                pe.wait_ge(s_xT, u)
            for i in range(TT):
                last = nc.tensor.transpose(ps_x[:, i * P:(i + 1) * P], x_rows[:, i, ct * P:(ct + 1) * P], ident[:])
            last.then_inc(s_x_tp, 1)

        def gates(b, e):
            for m in range(3):
                if e == 0 and m == 0:
                    pe.wait_ge(s_r1, b + 1)
                    if not first_batch(b):
                        pe.wait_ge(s_x2, CT * b)
                if e > 0:
                    pe.wait_ge(s_z, 12 * b + 3 * (e - 1) + m + 1)
                for dt in range(CT):
                    last = nc.tensor.matmul(ps_mm[:, m, :], wm[:, m, dt, e * P:(e + 1) * P],
                                            r1T[:, bass.ds(b % 2, 1), dt, :].rearrange("p o t -> p (o t)"),
                                            start=(dt == 0), stop=(dt == CT - 1))
                last.then_inc(s_mm, 1)

        def project(b):
            pe.wait_ge(s_y, b + 1)
            for e in range(CT):
                if e >= 3:
                    pe.wait_ge(s_x2, CT * b + e - 2)
                for dt in range(CT):
                    last = nc.tensor.matmul(ps_mm[:, e % 3, :], wm[:, 3, dt, e * P:(e + 1) * P], z_gate[:, dt, :],
                                            start=(dt == 0), stop=(dt == CT - 1))
                last.then_inc(s_wo, 1)

        def rows_out(b):
            first = first_batch(b)
            for i in range(TT):
                if i == 0:
                    pe.wait_ge(s_x2, CT * (b + 1))
                if i > 0:
                    pe.wait_ge(s_ev_x2, TT * b + i)
                elif not first:
                    pe.wait_ge(s_ev_r2, TT * b)
                for ct in range(CT):
                    last = nc.tensor.transpose(ps_to[:, ct * P:(ct + 1) * P], z_dec[:, ct, i * P:(i + 1) * P], ident[:])
                last.then_inc(s_to, 1)
            pe.wait_ge(s_r2, b + 1)
            for i in range(TT):
                for ct in range(CT):
                    last = nc.tensor.matmul(ps_logit[:, i, :], z_in[:, ct, i * P:(i + 1) * P], wg[:, ct, :],
                                            start=(ct == 0), stop=(ct == CT - 1))
            last.then_inc(s_logit, 1)
            for i in range(TT):
                if i == 0:
                    pe.wait_ge(s_ev_x2, TT * (b + 1))
                else:
                    pe.wait_ge(s_ev_r2, TT * b + i)
                for ct in range(CT):
                    last = nc.tensor.transpose(ps_to[:, ct * P:(ct + 1) * P], z_in[:, ct, i * P:(i + 1) * P], ident[:])
                last.then_inc(s_to, 1)
            pe.wait_ge(s_sel, b + 1)
            for i in range(TT):
                nc.tensor.matmul(ps_pos[:, i, :], lower[:], sel[:, i, :], start=True, stop=False)
                for j in range(i):
                    nc.tensor.matmul(ps_pos[:, i, :], ones[:], sel[:, j, :], start=False, stop=False)
                last = nc.tensor.matmul(ps_pos[:, i, :], ones[:], carry[:], start=False, stop=True)
            last.then_inc(s_pos, 1)

        pe.wait_ge(s_pool_setup, 8)
        pe.wait_ge(s_vec, 16 * N_VEC)
        nc.tensor.transpose(ps_small[:, 0:N_V * CT], vec_rows, ident[0:N_V * CT, 0:N_V * CT]).then_inc(s_vt, 1)

        def batch(b, with_gates):
            transpose_in(b, 0)
            transpose_in(b, 1)
            for e in range(CT):
                if with_gates:
                    gates(b - 1, e)
                if e + 2 < CT:
                    transpose_in(b, e + 2)

        pe.wait_ge(s_consts, 2)
        batch(0, False)
        pe.wait_ge(s_w, 16 * 5)
        batch(1, True)
        project(0)
        rows_out(0)
        with pe.Fori(2, B) as b:
            batch(b, True)
            project(b - 1)
            rows_out(b - 1)
        for e in range(CT):
            gates(B - 1, e)
        project(B - 1)
        rows_out(B - 1)
        pe.wait_ge(s_dest, B)
        nc.tensor.matmul(ps_count, ones[:], carry[:], start=True, stop=True).then_inc(s_count, 1)

    @block.scalar
    def _(act):
        a = nc.scalar

        def copy_in(b, ct):
            u = b * CT + ct
            act.wait_ge(s_f_tp, u + 1)
            if not isinstance(b, int) or u >= 2:
                act.wait_ge(s_eukv, u - 1)
            a.activation(kT[:, ct % 2], ps_f[:], ACT.Copy).then_inc(s_k, 1)
            act.wait_ge(s_x_tp, u + 1)
            if ct == 0 and (not isinstance(b, int) or b >= 2):
                act.wait_ge(s_r2, b - 1)
            a.activation(xT[:, bass.ds(b % 2, 1), ct, :], ps_x[:].rearrange("p (o t) -> p o t", o=1),
                         ACT.Copy).then_inc(s_xT, 1)

        def exps(b, ct):
            u, r = b * CT + ct, ct % 2
            act.wait_ge(s_caps, u + 1)
            a.activation(ek[:, r], ek[:, r], ACT.Exp).then_inc(s_ek, 1)
            a.activation(euk[:, r], euk[:, r], ACT.Exp).then_inc(s_euk, 1)

        def scale(b, ct):
            u, r = b * CT + ct, ct % 2
            act.wait_ge(s_bwd, u + 1)
            if not isinstance(b, int) or u >= 1:
                act.wait_ge(s_den, u)
            for c in range(2):
                last = a.activation(scaled[:, c, :, 1:T], sums[:, r, c, :, 1:T], ACT.Copy, scale=one_md2[:, col(b, c, ct)])
            last.then_inc(s_scaled, 1)

        def first_reciprocal(b, ct):
            u, r = b * CT + ct, ct % 2
            act.wait_ge(s_den, u + 1)
            if not isinstance(b, int) or u >= 1:
                act.wait_ge(s_newton, 2 * u)
            for c in range(2):
                a.activation(recip0[:, c], sums[:, r, c, 1], ACT.Ln).then_inc(s_ln, 1)
            for c in range(2):
                act.wait_ge(s_ln, 2 * u + c + 1)
                a.activation(recip0[:, c], recip0[:, c], ACT.Exp, scale=-1.0).then_inc(s_rec, 1)

        def gate_sums(b, e):
            if e == 0 and not first_batch(b):
                act.wait_ge(s_to, 2 * TT * b)
            for m, (z, bias) in enumerate(((z_in, vec[:, BIN, e:e + 1]), (z_dec, bdec[:, e:e + 1]),
                                           (z_gate, vec[:, BGATE, e:e + 1]))):
                act.wait_ge(s_mm, 12 * b + 3 * e + m + 1)
                a.activation(z[:, e], ps_mm[:, m, :], ACT.Identity, bias=bias).then_inc(s_z, 1)

        def gate_functions(b):
            act.wait_ge(s_z, 12 * (b + 1))
            a.activation(z_in[:], z_in[:], ACT.Silu)
            a.activation(z_dec[:], z_dec[:], ACT.Sigmoid)
            a.activation(z_gate[:], z_gate[:], ACT.Sigmoid).then_inc(s_gates, 1)

        def sigmoid_x(b):
            if not isinstance(b, int) or b >= 2:
                act.wait_ge(s_r2, b - 1)
            act.wait_ge(s_xT, CT * (b + 1))
            act.nop(nofuse=True)
            a.activation(sig[:], xT[:, bass.ds(b % 2, 1)].rearrange("p o c t -> p (o c) t"), ACT.Sigmoid).then_inc(s_sig1, 1)

        def tail(b, r1_done):
            act.wait_ge(s_x2, CT * (b + 1))
            act.wait_ge(s_r1, r1_done)
            a.activation(sig[:], z_dec[:], ACT.Sigmoid).then_inc(s_sig2, 1)
            if not (first_batch(b)):
                act.wait_ge(s_x2_out, 16 * b)
            for i in range(TT):
                act.wait_ge(s_to, 2 * TT * b + i + 1)
                a.activation(x2_rows[:, i], ps_to[:], ACT.Copy).then_inc(s_ev_x2, 1)
            if first_batch(b):
                act.wait_ge(s_init, 16 * (NE + 1) * ST)
            else:
                act.wait_ge(s_disp, 16 * TT * TOPK * b)
            for i in range(TT):
                act.wait_ge(s_to, 2 * TT * b + TT + i + 1)
                a.activation(r2_rows[:, i, 0:C], ps_to[:], ACT.Copy).then_inc(s_ev_r2, 1)
            act.wait_ge(s_shift, b + 1)
            a.activation(pe_[:], pe_[:], ACT.Exp).then_inc(s_pexp, 1)

        def conditioning(b, with_gates):
            copy_in(b, 0)
            for s in range(CT + 1):
                if s < CT:
                    exps(b, s)
                if s + 1 < CT:
                    copy_in(b, s + 1)
                if with_gates and s < CT:
                    gate_sums(b - 1, s)
                if s >= 1:
                    first_reciprocal(b, s - 1)
                if s < CT:
                    scale(b, s)
            if with_gates:
                gate_functions(b - 1)
            sigmoid_x(b)

        act.wait_ge(s_setup_v, 1)
        setup = Steps(act, s_setup_a, 0)
        setup.do(a.activation(ew[:], vec[:, W1C:W2C + 1, :], ACT.Exp))
        setup.do(a.activation(ew[:], ew[:], ACT.Exp, scale=-1.0))
        act.wait_ge(s_setup_v, 2)
        setup.do(a.activation(tf[:], tf[:], ACT.Sigmoid))
        act.wait_ge(s_consts, 2)
        conditioning(0, False)
        conditioning(1, True)
        tail(0, 2)
        with act.Fori(2, B) as b:
            conditioning(b, True)
            tail(b - 1, b + 1)
        for e in range(CT):
            gate_sums(B - 1, e)
        gate_functions(B - 1)
        tail(B - 1, B)

    @block.vector
    def _(dve):
        v = nc.vector
        d0 = lambda b, c, ct, n: ps_decay[:, col(b, c, ct)].to_broadcast([P, n])

        setup = Steps(dve, s_setup_v, 0)
        dve.wait_ge(s_vt, 1)
        setup.do(v.tensor_copy(vec[:].rearrange("p n t -> p (n t)"), ps_small[:, 0:N_V * CT]))
        dve.wait_ge(s_vec, 16 * N_VEC)
        setup.mark(v.tensor_reduce(tf[:], vec_cond.rearrange("p (b d) -> p b d", b=B), AX.X, ALU.add))
        setup.mark(v.tensor_tensor(bdec[:], vec[:, BDEC], vec[:, DBIAS], ALU.add))
        dve.wait_ge(s_setup_a, 3)
        setup.mark(v.tensor_scalar(half_tf[:], tf[:], 0.5, 0.5, ALU.mult, ALU.add))
        setup.mark(v.tensor_scalar(neg_scale[:], tf[:], 0.2, 0.8, ALU.mult, ALU.add))
        setup.wait()
        setup.mark(v.tensor_scalar(neg_scale[:], neg_scale[:], -1.0, None, ALU.mult))
        for b in range(B):
            setup.mark(v.tensor_scalar(decay[:, b * 2 * CT:(b + 1) * 2 * CT], ew[:].rearrange("p c t -> p (c t)"),
                                       half_tf[:, b:b + 1], None, ALU.mult))
        setup.wait()
        setup.mark(v.tensor_copy(ps_decay, decay[:]))
        setup.mark(v.tensor_scalar(one_m[:], decay[:], -1.0, 1.0, ALU.mult, ALU.add))
        setup.wait()
        v.scalar_tensor_tensor(out=one_md2[:], in0=decay[:], scalar=1.0, in1=one_m[:], op0=ALU.add,
                               op1=ALU.mult).then_inc(s_consts, 1)
        v.memset(r2_rows[:], 0.0).then_inc(s_template, 1)
        dve.wait_ge(s_template, 1)
        v.memset(r2_rows[:, 0, C + NE:ROW].bitcast(U32), NO_TOKEN).then_inc(s_template, 1)

        def caps(b, ct):
            u, r = b * CT + ct, ct % 2
            dve.wait_ge(s_k, u + 1)
            v.tensor_scalar(ek[:, r], kT[:, r], CAPV, None, ALU.min)
            for c in range(2):
                last = v.tensor_scalar(euk[:, r, c], kT[:, r], vec[:, U1C + c, ct:ct + 1], CAPV, ALU.add, ALU.min)
            last.then_inc(s_caps, 1)

        def backward(b, ct):
            u, r = b * CT + ct, ct % 2
            dve.wait_ge(s_ek, u + 1)
            for c in range(2):
                v.tensor_tensor_scan(sums[:, r, c, 1, ::-1], d0(b, c, ct, T), ek[:, r, ::-1], 0.0, ALU.mult, ALU.add)
            dve.wait_ge(s_ekv, u + 1)
            for c in range(2):
                last = v.tensor_tensor_scan(sums[:, r, c, 0, ::-1], d0(b, c, ct, T), ekv[:, r, ::-1], 0.0, ALU.mult, ALU.add)
            last.then_inc(s_bwd, 1)

        def fold(b, ct):
            u, r = b * CT + ct, ct % 2
            steps = Steps(dve, s_fold, 6 * u)
            dve.wait_ge(s_scaled, u + 1)
            for c in range(2):
                for n in range(2):
                    s = sums[:, r, c, n]
                    ins = v.tensor_tensor_scan(s[:, 1:T], d0(b, c, ct, T - 1), scaled[:, c, n, 1:T], s[:, 0:1], ALU.mult, ALU.add)
                    if n == 1:
                        steps.mark(ins)
            steps.wait()
            steps.mark(v.tensor_tensor(sums[:, r, 0, 1], sums[:, r, 0, 1], euk[:, r, 0], ALU.add))
            steps.mark(v.tensor_tensor(sums[:, r, 1, 1], sums[:, r, 1, 1], euk[:, r, 1], ALU.add))
            dve.wait_ge(s_eukv, u + 1)
            steps.mark(v.tensor_tensor(sums[:, r, 0, 0], sums[:, r, 0, 0], eukv[:, r, 0], ALU.add))
            steps.do(v.tensor_tensor(sums[:, r, 1, 0], sums[:, r, 1, 0], eukv[:, r, 1], ALU.add))
            v.tensor_scalar(sums[:, r, :, 1], sums[:, r, :, 1], DEN_MIN, None, ALU.max).then_inc(s_den, 1)

        def ratio(b, ct):
            u, r = b * CT + ct, ct % 2
            for c, dst in enumerate((r1T, ratio2)):
                dve.wait_ge(s_newton, 2 * u + c + 1)
                if c == 0 and ct == 0 and not isinstance(b, int):
                    dve.wait_ge(s_mm, 12 * (b - 1))
                last = v.scalar_tensor_tensor(out=dst[:, bass.ds(b % 2, 1), ct, :],
                                              in0=sums[:, r, c, 1].rearrange("p (o t) -> p o t", o=1), scalar=2.0,
                                              in1=sums[:, r, c, 0].rearrange("p (o t) -> p o t", o=1),
                                              op0=ALU.subtract, op1=ALU.mult)
            last.then_inc(s_ratio, 1)

        def conditioning(b):
            for s in range(CT + 2):
                if s < CT:
                    caps(b, s)
                if 2 <= s:
                    ratio(b, s - 2)
                if 1 <= s <= CT:
                    fold(b, s - 1)
                if s < CT:
                    backward(b, s)

        def first_out(b):
            dve.wait_ge(s_sig1, b + 1)
            dve.wait_ge(s_ratio, CT * (b + 1))
            r1 = r1T[:, bass.ds(b % 2, 1)].rearrange("p o c t -> p (o c) t")
            v.scalar_tensor_tensor(out=r1, in0=r1, scalar=neg_scale[:, bass.ds(b, 1)], in1=sig[:],
                                   op0=ALU.mult, op1=ALU.mult).then_inc(s_r1, 1)

        def recurrence(b):
            steps = Steps(dve, s_rec_steps, (1 + CT) * b)
            dve.wait_ge(s_gates, b + 1)
            steps.do(v.scalar_tensor_tensor(out=z_in[:], in0=z_dec[:], scalar=1.0, in1=z_in[:],
                                            op0=ALU.subtract, op1=ALU.mult))
            for e in range(CT):
                steps.mark(v.tensor_tensor_scan(z_in[:, e], z_dec[:, e], z_in[:, e], 0.0, ALU.mult, ALU.subtract))
            steps.wait()
            v.tensor_tensor(z_gate[:], z_gate[:], z_in[:], ALU.mult).then_inc(s_y, 1)

        def residual(b):
            for e in range(CT):
                dve.wait_ge(s_wo, CT * b + e + 1)
                if e == 0:
                    dve.wait_ge(s_y, b + 1)
                v.scalar_tensor_tensor(out=z_dec[:, e:e + 1], in0=ps_mm[:, e % 3:e % 3 + 1, :], scalar=vec[:, BOUT, e:e + 1],
                                       in1=xT[:, bass.ds(b % 2, 1), e, :], op0=ALU.add, op1=ALU.add).then_inc(s_x2, 1)
            dve.wait_ge(s_sig2, b + 1)
            v.scalar_tensor_tensor(out=z_in[:], in0=ratio2[:, bass.ds(b % 2, 1)].rearrange("p o c t -> p (o c) t"),
                                   scalar=neg_scale[:, bass.ds(b, 1)], in1=sig[:],
                                   op0=ALU.mult, op1=ALU.mult).then_inc(s_r2, 1)

        def route(b):
            st = Steps(dve, s_route, ROUTE_STEPS * b)
            bc = lambda ap: ap.to_broadcast([P, TT, NE])
            dve.wait_ge(s_logit, b + 1)
            st.do(v.tensor_copy(logit[:], ps_logit))
            dve.nop(nofuse=True)
            for i in range(TT):
                st.mark(v.max(top[:, i], logit[:, i]))
            st.wait()
            v.tensor_tensor(pe_[:], logit[:], bc(top[:, :, 0:1]), ALU.subtract).then_inc(s_shift, 1)
            for i in range(TT):
                st.mark(v.max_index(top_i[:, i], top[:, i], logit[:, i]))
            st.wait()
            st.do(v.tensor_copy(top_f[:], top_i[:]))
            for k in range(TOPK):
                st.mark(v.tensor_tensor(oh[:, k], expert_no[:], bc(top_f[:, :, k:k + 1]), ALU.is_equal))
            st.wait()
            v.tensor_tensor(sel[:], oh[:, 0], oh[:, 1], ALU.add).then_inc(s_sel, 1)
            dve.wait_ge(s_sel, b + 1)
            st.mark(v.tensor_reduce(sel_sum[:], sel[:].rearrange("p i e -> p e i"), AX.X, ALU.add))
            dve.wait_ge(s_ev_r2, TT * (b + 1))
            st.mark(v.tensor_copy(r2_rows[:, :, C + NE:ROW].bitcast(U32),
                                  token_no[:, bass.ds(b * TT, TT)].rearrange("p (i o) -> p i o", o=1)))
            dve.wait_ge(s_pexp, b + 1)
            st.do(v.tensor_reduce(psum_[:], pe_[:], AX.X, ALU.add))
            st.do(v.reciprocal(psum_[:], psum_[:]))
            st.mark(v.tensor_tensor(r2_rows[:, :, C:C + NE], pe_[:], bc(psum_[:].rearrange("p (i o) -> p i o", o=1)), ALU.mult))
            dve.wait_ge(s_pos, b + 1)
            st.do(v.tensor_scalar(slot_t[:], ps_pos, float(CAP), float(NO_TOKEN), ALU.is_ge, ALU.mult))
            st.do(v.tensor_tensor(slot_f[:], ps_pos, slot_t[:], ALU.add))
            st.do(v.tensor_tensor(slot_f[:], slot_f[:], slot_base[:], ALU.add))
            for k in range(TOPK):
                st.do(v.tensor_tensor(slot_t[:], slot_f[:], oh[:, k], ALU.mult))
                st.do(v.tensor_reduce(dest_f[:, k], slot_t[:], AX.X, ALU.add))
            st.do(v.tensor_tensor(carry[:], carry[:], sel_sum[:], ALU.add))
            if not (first_batch(b)):
                dve.wait_ge(s_disp, 16 * TT * TOPK * b)
            v.tensor_copy(dest[:], dest_f[:]).then_inc(s_dest, 1)
            assert st.n == ROUTE_STEPS, st.n

        dve.wait_ge(s_consts, 2)
        dve.wait_ge(s_pool_setup, 8)
        conditioning(0)
        first_out(0)
        conditioning(1)
        recurrence(0)
        first_out(1)
        residual(0)
        route(0)
        with dve.Fori(2, B) as b:
            conditioning(b)
            recurrence(b - 1)
            first_out(b)
            residual(b - 1)
            route(b - 1)
        recurrence(B - 1)
        residual(B - 1)
        route(B - 1)
        dve.wait_ge(s_count, 1)
        v.tensor_copy(counts[:], ps_count).then_inc(s_count, 1)
        dve.wait_ge(s_count, 2)


def experts(nc, ctx, ident, counts, slots, out_rows, w1, w2):
    def sb(name, shape, dt=F32):
        return ctx.enter_context(nc.sbuf_tensor(name, shape, dt))

    def ps(name, shape, dt=F32):
        return ctx.enter_context(nc.psum_tensor(name, shape, dt))

    def sem(name):
        return ctx.enter_context(nc.semaphore(name))

    FW = FC * P
    raw1 = sb("raw1", [P, 2, CT, FW])
    raw2 = sb("raw2", [P, 2, FC, C])
    w1h, w1l = sb("w1h", [P, 2, CT, FW], F32R), sb("w1l", [P, 2, CT, FW], F32R)
    w2h, w2l = sb("w2h", [P, 2, FC, C], F32R), sb("w2l", [P, 2, FC, C], F32R)
    rows = sb("rows", [P, ST, ROW])
    xh, xl = sb("xh", [P, 2, CT, CAP], F32R), sb("xl", [P, 2, CT, CAP], F32R)
    hh, hl = sb("hh", [P, 2, CAP], F32R), sb("hl", [P, 2, CAP], F32R)
    y = sb("y", [P, ST, C])
    gate = sb("gate", [P, ST])
    token = sb("token", [P, ST], U32)

    ps_y = ps("ps_y", [P, ST, C])
    ps_h = ps("ps_h", [P, 2, 512])
    ps_t = ps("ps_t", [P, CT, P])

    s_w, s_rows = [sem("weights_in_even"), sem("weights_in_odd")], sem("rows_in")
    s_wh, s_wl = sem("weights_high"), sem("weights_low")
    s_tp, s_xh, s_xl = sem("rows_transposed2"), sem("x_high"), sem("x_low")
    s_h, s_hh, s_hl, s_f = sem("hidden_done"), sem("hidden_high"), sem("hidden_low"), sem("hidden_used")
    s_y, s_ya, s_yv = sem("y_done"), sem("y_even"), sem("y_odd")
    s_gate, s_token, s_add = sem("gate_ready"), sem("token_ready"), sem("rows_added")
    s_y0 = sem("y_cleared")

    SPLIT_AT = {0: range(0, 0), 1: range(0, 3), 2: range(3, 7), 3: range(7, 8)}
    TURN_AT = {3: 0, 5: 1, 7: 2, 9: 3, 11: 4}
    CLASSES = (3, 4, 5)

    def piece(n, high, low, ring):
        if n < CT:
            return high[0][:, ring, n], low[0][:, ring, n], raw1[:, ring, n]
        return high[1][:, ring, n - CT], low[1][:, ring, n - CT], raw2[:, ring, n - CT]

    def by_class(eng, e, body):
        n = eng.value_load(counts[0:1, bass.ds(e, 1)], min_val=0, max_val=B * T)
        with eng.If(n < CLASSES[0] * P + 1):
            body(CLASSES[0])
        with eng.Else():
            with eng.If(n < CLASSES[1] * P + 1):
                body(CLASSES[1])
            with eng.Else():
                body(CLASSES[2])

    block = ctx.enter_context(nc.Block())

    @block.sync
    def _(sp):
        def weights(e, c):
            sp.dma_start(raw1[:, c % 2], w1[bass.ds(e, 1), :, c * FW:(c + 1) * FW].rearrange("o (t p) f -> p (o t) f", p=P)).then_inc(s_w[c % 2], 16)
            sp.dma_start(raw2[:, c % 2], w2[bass.ds(e, 1), c * FW:(c + 1) * FW, :].rearrange("o (t p) n -> p (o t) n", p=P)).then_inc(s_w[c % 2], 16)

        def load_rows(e):
            sp.dma_start(rows[:], slots[bass.ds(e * CAP, CAP)].rearrange("(i p) c -> p i c", p=P)).then_inc(s_rows, 16)

        def expert(e):
            for c in range(NC):
                if not (isinstance(e, int) and c < 2):
                    sp.wait_ge(s_wl, PIECES * (e * NC + (c - 1)))
                weights(e, c)
                if c == 1:
                    sp.wait_ge(s_tp, ST * (e + 1))
                    sp.wait_ge(s_gate, e + 1)
                    sp.wait_ge(s_token, e + 1)
                    load_rows(e + 1)

        load_rows(0)
        expert(0)
        with sp.Fori(1, NE) as e:
            expert(e)
        sp.wait_ge(s_wl, PIECES * (NE * NC - 1))
        weights(0, 0)
        sp.wait_ge(s_w[0], 32 * (NE * NC // 2 + 1))
        sp.wait_ge(s_w[1], 32 * (NE * NC // 2))
        sp.wait_ge(s_rows, 16 * (NE + 1))

    @block.gpsimd
    def _(pool):
        nc.gpsimd.memset(y[:], 0.0).then_inc(s_y0, 1)
        def expert(e, first):
            pool.wait_ge(s_rows, 16 * (e + 1))
            if not first:
                pool.wait_ge(s_add, 16 * ST * e)
            pool.nop(nofuse=True)
            nc.gpsimd.tensor_copy(token[:], rows[:, :, C + NE:ROW].bitcast(U32).rearrange("p i o -> p (i o)")).then_inc(s_token, 1)
            pool.wait_ge(s_token, e + 1)
            pool.wait_ge(s_ya, e + 2)
            pool.wait_ge(s_yv, e + 2)
            pool.wait_ge(s_y0, 1)
            pool.nop(nofuse=True)
            for i in range(ST):
                pool.indirect_dma_start(
                    out=out_rows, out_offset=bass.IndirectOffsetOnAxis(ap=token[:, i:i + 1], axis=0),
                    in_=y[:, i, :], in_offset=None, bounds_check=B * T - 1, oob_is_err=False,
                    compute_op=ALU.add).then_inc(s_add, 16)
        expert(0, True)
        with pool.Fori(1, NE) as e:
            expert(e, False)
        pool.wait_ge(s_add, 16 * ST * NE)

    @block.tensor
    def _(pe):
        def turn(e, i):
            pe.wait_ge(s_rows, 16 * (e + 1))
            if not (isinstance(e, int) and i == 0):
                pe.wait_ge(s_xl, ST * e + i)
            for ct in range(CT):
                last = nc.tensor.transpose(ps_t[:, ct, :], rows[:, i, ct * P:(ct + 1) * P], ident[:])
            last.then_inc(s_tp, 1)

        def up(e, par, f, t):
            g = e * NC + f // FC
            if f % FC == 0:
                pe.wait_ge(s_wl, PIECES * (g + 1))
            if f == 0:
                pe.wait_ge(s_xl, ST * (e + 1))
            hidden = e * FT + f
            pe.wait_ge(s_hl, hidden + 1)
            r, j = (f // FC) % 2, f % FC
            parts = ((0, t * P // 2), (t * P // 2, t * P)) if t * P > 512 else ((0, t * P),)
            for n, (lo, hi) in enumerate(parts):
                for dt in range(CT):
                    wcol = slice(j * P, (j + 1) * P)
                    o = ps_h[:, n, 0:hi - lo]
                    nc.tensor.matmul(o, w1h[:, r, dt, wcol], xh[:, par, dt, lo:hi], start=(dt == 0), stop=False)
                    nc.tensor.matmul(o, w1h[:, r, dt, wcol], xl[:, par, dt, lo:hi], start=False, stop=False)
                    last = nc.tensor.matmul(o, w1l[:, r, dt, wcol], xh[:, par, dt, lo:hi], start=False, stop=(dt == CT - 1))
            last.then_inc(s_h, 1)

        def down(e, f, t):
            if f == 0:
                pe.wait_ge(s_ya, e + 1)
                pe.wait_ge(s_yv, e + 1)
            pe.wait_ge(s_hl, e * FT + f + 2)
            r, j = (f // FC) % 2, f % FC
            for i in range(t):
                tok = slice(i * P, (i + 1) * P)
                nc.tensor.matmul(ps_y[:, i, :], hh[:, f % 2, tok], w2h[:, r, j], start=(f == 0), stop=False)
                nc.tensor.matmul(ps_y[:, i, :], hl[:, f % 2, tok], w2h[:, r, j], start=False, stop=False)
                last = nc.tensor.matmul(ps_y[:, i, :], hh[:, f % 2, tok], w2l[:, r, j], start=False, stop=(f == FT - 1))
            last.then_inc(s_y if f == FT - 1 else s_f, 1)

        for i in range(ST):
            turn(0, i)
        with pe.Fori(0, NE // 2) as pair:
            for par in range(2):
                e = pair * 2 + par

                def body(t):
                    up(e, par, 0, t)
                    for f in range(FT):
                        if f + 1 < FT:
                            up(e, par, f + 1, t)
                        if f in TURN_AT:
                            turn(e + 1, TURN_AT[f])
                        down(e, f, t)
                by_class(pe, e, body)

    @block.scalar
    def _(act):
        a = nc.scalar

        def token_high(e, par, i):
            act.wait_ge(s_tp, ST * e + i + 1)
            a.activation(xh[:, par, :, i * P:(i + 1) * P], ps_t[:], ACT.Copy).then_inc(s_xh, 1)

        def weight_high(e, c, n):
            ring = c % 2
            if n == 0:
                act.wait_ge(s_w[ring], 32 * (e * (NC // 2) + (c // 2 + 1)))
            h, _, raw = piece(n, (w1h, w2h), (w1l, w2l), ring)
            a.activation(h, raw, ACT.Copy).then_inc(s_wh, 1)

        act.sem_inc(s_ya, 1)
        for n in range(PIECES):
            weight_high(0, 0, n)
        for i in range(ST):
            token_high(0, 0, i)
        with act.Fori(0, NE // 2) as pair:
            for par in range(2):
                e = pair * 2 + par

                def body(t):
                    for f in range(FT):
                        hidden = e * FT + f
                        act.wait_ge(s_h, hidden + 1)
                        if f >= 2:
                            act.wait_ge(s_f, e * (FT - 1) + (f - 1))
                        half = t * P // 2
                        if t * P > 512:
                            a.activation(hh[:, f % 2, 0:t * P].rearrange("p (n s) -> p n s", n=2), ps_h[:, :, 0:half], ACT.Relu).then_inc(s_hh, 1)
                        else:
                            a.activation(hh[:, f % 2, 0:t * P], ps_h[:, 0, 0:t * P], ACT.Relu).then_inc(s_hh, 1)
                        c = f // FC
                        for n in SPLIT_AT[f % FC]:
                            if n == 0 and c > 0:
                                act.wait_ge(s_f, e * (FT - 1) + c * FC)
                            weight_high(e, c + 1, n)
                        if f in TURN_AT:
                            token_high(e + 1, 1 - par, TURN_AT[f])
                    act.wait_ge(s_y, e + 1)
                    act.wait_ge(s_gate, e + 1)
                    act.wait_ge(s_y0, 1)
                    act.wait_ge(s_token, e + 1)
                    for i in range(0, t, 2):
                        last = a.activation(y[:, i], ps_y[:, i, :], ACT.Copy, scale=gate[:, i:i + 1])
                    last.then_inc(s_ya, 1)
                by_class(act, e, body)

    @block.vector
    def _(dve):
        v = nc.vector

        def token_low(e, par, i):
            dve.wait_ge(s_xh, ST * e + i + 1)
            s = slice(i * P, (i + 1) * P)
            v.tensor_tensor(xl[:, par, :, s], ps_t[:], xh[:, par, :, s].bitcast(F32), ALU.subtract).then_inc(s_xl, 1)

        def weight_low(g, ring, n):
            dve.wait_ge(s_wh, PIECES * g + n + 1)
            h, l, raw = piece(n, (w1h, w2h), (w1l, w2l), ring)
            v.tensor_tensor(l, raw, h.bitcast(F32), ALU.subtract).then_inc(s_wl, 1)

        dve.sem_inc(s_hl, 1)
        dve.sem_inc(s_yv, 1)
        for n in range(PIECES):
            weight_low(0, 0, n)
        for i in range(ST):
            token_low(0, 0, i)
        with dve.Fori(0, NE // 2) as pair:
            for par in range(2):
                e = pair * 2 + par
                dve.wait_ge(s_rows, 16 * (e + 1))
                dve.wait_ge(s_ya, e + 1)
                dve.wait_ge(s_yv, e + 1)
                v.tensor_copy(gate[:], rows[:, :, bass.ds(e + C, 1)].rearrange("p i o -> p (i o)")).then_inc(s_gate, 1)

                def body(t):
                    for f in range(FT):
                        dve.wait_ge(s_hh, e * FT + f + 1)
                        half = t * P // 2
                        if t * P > 512:
                            o, src, high = (z.rearrange("p (n s) -> p n s", n=2) if k else z for k, z in
                                            ((1, hl[:, f % 2, 0:t * P]), (0, ps_h[:, :, 0:half]), (1, hh[:, f % 2, 0:t * P].bitcast(F32))))
                        else:
                            o, src, high = hl[:, f % 2, 0:t * P], ps_h[:, 0, 0:t * P], hh[:, f % 2, 0:t * P].bitcast(F32)
                        v.scalar_tensor_tensor(out=o, in0=src, scalar=0.0, in1=high, op0=ALU.max, op1=ALU.subtract).then_inc(s_hl, 1)
                        c = f // FC
                        for n in SPLIT_AT[f % FC]:
                            weight_low(e * NC + (c + 1), (c + 1) % 2, n)
                        if f in TURN_AT:
                            token_low(e + 1, 1 - par, TURN_AT[f])
                    dve.wait_ge(s_y, e + 1)
                    dve.wait_ge(s_gate, e + 1)
                    dve.wait_ge(s_y0, 1)
                    dve.wait_ge(s_token, e + 1)
                    for i in range(1, t, 2):
                        last = v.tensor_scalar(y[:, i], ps_y[:, i, :], gate[:, i:i + 1], None, ALU.mult)
                    last.then_inc(s_yv, 1)
                by_class(dve, e, body)


_INS = ["x", "fside_BxSxS_0", "cond_512", "L0_cond_w", "L0_cond_u", "L0_attn_W_in", "L0_attn_b_in",
        "L0_attn_W_decay", "L0_attn_b_decay", "L0_attn_W_gate", "L0_attn_b_gate", "L0_attn_W_out",
        "L0_attn_b_out", "L0_attn_decay_bias", "L0_cond2_w", "L0_cond2_u", "L0_ffn_Wg", "L0_ffn_w1", "L0_ffn_w2"]


def kernel(**inputs):
    import numpy as _np
    import concourse.bacc as _bacc
    from concourse import mybir as _mybir
    from concourse.bass_utils import run_bass_kernel_spmd as _run

    nc = _bacc.Bacc("TRN2", target_bir_lowering=False, num_devices=1)
    arrays, args = {}, []
    for name in _INS:
        a = _np.ascontiguousarray(inputs[name])
        arrays[f"in_{name}_dram"] = a
        args.append(nc.dram_tensor(f"in_{name}_dram", a.shape, _mybir.dt.from_np(a.dtype), kind="ExternalInput").ap())
    args.append(nc.dram_tensor("out_0_dram", (B, T, C), _mybir.dt.float32, kind="ExternalOutput").ap())
    build_program(nc, *args)
    r = _run(nc, [arrays], core_ids=[0])
    return r.results[0]["out_0_dram"]
```

```python
from contextlib import ExitStack
import math

import concourse.bass as bass
from concourse import mybir

F32 = mybir.dt.float32
F32R = mybir.dt.float32r
BF16 = mybir.dt.bfloat16
I32 = mybir.dt.int32
U32 = mybir.dt.uint32
ALU = mybir.AluOpType
ACT = mybir.ActivationFunctionType
AX = mybir.AxisListType

P = 128
B, T, C = 4, 512, 512
CT = C // P
TT = T // P
NE, DFF, TOPK = 8, 2048, 2
CAP = math.ceil(1.25 * B * T * TOPK / NE)
ST = CAP // P
ROW = C + NE + 1
NO_TOKEN = 1 << 20
CAPV, DEN_MIN = 30.0, 1e-8
FT = DFF // P
FC = 4
NC = FT // FC
PIECES = 2 * FC
W1C, W2C, U1C, U2C, BIN, BGATE, BOUT, BDEC, DBIAS = range(9)


GATE_TILES = [(0, e) for e in range(CT)] + [(m, e) for e in range(CT) for m in (1, 2)]
IN_PSUM = 2
Z_COPIES = len(GATE_TILES) - IN_PSUM


def first_batch(b):
    return isinstance(b, int) and b == 0


def at_least(b, n):
    return not isinstance(b, int) or b >= n


class Steps:

    def __init__(self, eng, sem, base):
        self.eng, self.sem, self.base, self.n = eng, sem, base, 0

    def mark(self, ins):
        ins.then_inc(self.sem, 1)
        self.n += 1

    def wait(self):
        self.eng.wait_ge(self.sem, self.base + self.n)

    def do(self, ins):
        self.mark(ins)
        self.wait()


def build_program(nc, x, fside, cond, w1c, u1c, W_in, b_in, W_decay, b_decay, W_gate, b_gate,
                  W_out, b_out, decay_bias, w2c, u2c, Wg, w1, w2, out):
    slots = nc.dram_tensor("slots", ((NE + 1) * CAP, ROW), F32, kind="Internal").ap()
    out_rows = out.rearrange("b t c -> (b t) c")
    with ExitStack() as ctx:
        def sb(name, shape, dt=F32):
            return ctx.enter_context(nc.sbuf_tensor(name, shape, dt))

        ident = sb("ident", [P, P])
        counts = sb("counts", [P, NE], I32)
        with ExitStack() as phase:
            conditioning_and_routing(nc, phase, ident, counts, slots, out_rows, x, fside, cond, w1c, u1c,
                                     W_in, b_in, W_decay, b_decay, W_gate, b_gate, W_out, b_out,
                                     decay_bias, w2c, u2c, Wg)
        with ExitStack() as phase:
            experts(nc, phase, ident, counts, slots, out_rows, w1, w2)


def conditioning_and_routing(nc, ctx, ident, counts, slots, out_rows, x, fside, cond, w1c, u1c,
                             W_in, b_in, W_decay, b_decay, W_gate, b_gate, W_out, b_out,
                             decay_bias, w2c, u2c, Wg):
    def sb(name, shape, dt=F32):
        return ctx.enter_context(nc.sbuf_tensor(name, shape, dt))

    def ps(name, shape, dt=F32):
        return ctx.enter_context(nc.psum_tensor(name, shape, dt))

    def sem(name):
        return ctx.enter_context(nc.semaphore(name))

    lower = sb("lower", [P, P], BF16)
    ones = sb("ones", [P, P], BF16)
    expert_no = sb("expert_no", [P, TT, NE])
    slot_base = sb("slot_base", [P, TT, NE])
    token_no = sb("token_no", [P, B * TT], U32)
    vec = sb("vec", [P, 9, CT])
    wm = sb("wm", [P, 4, CT, C])
    wg = sb("wg", [P, CT, NE])
    tf = sb("tf", [P, B])
    half_tf = sb("half_tf", [P, B])
    neg_scale = sb("neg_scale", [P, B])
    ew = sb("ew", [P, 2, CT])
    decay = sb("decay", [P, B * 2 * CT])
    one_m = sb("one_m", [P, B * 2 * CT])
    one_md2 = sb("one_md2", [P, B * 2 * CT])
    bdec = sb("bdec", [P, CT])
    x_rows = sb("x_rows", [P, TT, C])
    f_rows = sb("f_rows", [P, TT, C])
    xT = sb("xT", [P, 2, CT, T])
    kT = sb("kT", [P, 2, T])
    ek = sb("ek", [P, 2, T])
    ekv = sb("ekv", [P, 2, T])
    euk = sb("euk", [P, 2, 2, T])
    eukv = sb("eukv", [P, 2, 2, T])
    sums = sb("sums", [P, 2, 2, 2, T])
    scaled = sb("scaled", [P, 2, 2, T])
    recip0 = sb("recip0", [P, 2, T])
    r1T = sb("r1T", [P, 2, CT, T])
    ratio2 = sb("ratio2", [P, 2, CT, T])
    sig = sb("sig", [P, CT, T])
    z_in = sb("z_in", [P, CT, T])
    z_dec = sb("z_dec", [P, CT, T])
    z_gate = sb("z_gate", [P, CT, T])
    x2_rows = sb("x2_rows", [P, TT, C])
    r2_rows = sb("r2_rows", [P, TT, ROW])
    logit = sb("logit", [P, TT, NE])
    top = sb("top", [P, TT, NE])
    top_i = sb("top_i", [P, TT, NE], U32)
    top_f = sb("top_f", [P, TT, NE])
    oh = sb("oh", [P, 2, TT, NE])
    sel = sb("sel", [P, TT, NE], BF16)
    carry = sb("carry", [P, NE], BF16)
    sel_sum = sb("sel_sum", [P, NE])
    pe_ = sb("prob", [P, TT, NE])
    psum_ = sb("prob_sum", [P, TT])
    slot_f = sb("slot_f", [P, TT, NE])
    slot_t = sb("slot_t", [P, TT, NE])
    dest_f = sb("dest_f", [P, 2, TT])
    dest = sb("dest", [P, 2, TT], U32)

    ps_f = ps("ps_f", [P, T])
    ps_x = ps("ps_x", [P, T])
    ps_mm = ps("ps_mm", [P, 3, T])
    bank = lambda e: ps_x[:] if e == 1 else ps_mm[:, (0, None, 1, 2)[e], :]
    ps_to = ps("ps_to", [P, C])
    ps_small = ps("ps_small", [P, 512])
    ps_logit = ps_small[:, 0:32].rearrange("p (i e) -> p i e", i=TT)
    ps_pos = ps_small[:, 32:64].rearrange("p (i e) -> p i e", i=TT)
    ps_count = ps_small[:, 64:72]
    ps_decay = ps("ps_decay", [P, 512])[:, 0:B * 2 * CT]

    s_vec, s_w, s_f_in, s_x_in = sem("vec_in"), sem("w_in"), sem("f_in"), sem("x_in")
    s_init, s_x2_out, s_disp = sem("slots_init"), sem("x2_out"), sem("dispatched")
    s_pool_setup, s_template, s_consts = sem("pool_setup"), sem("template"), sem("consts_ready")
    s_setup_v, s_setup_a = sem("setup_dve"), sem("setup_act")
    s_f_tp, s_x_tp, s_k, s_xT = sem("f_transposed"), sem("x_transposed"), sem("k_ready"), sem("xT_ready")
    s_caps, s_ek, s_euk, s_ekv, s_eukv = sem("caps_ready"), sem("ek_ready"), sem("euk_ready"), sem("ekv_ready"), sem("eukv_ready")
    s_bwd, s_scaled, s_den, s_ln, s_rec, s_newton, s_ratio = (
        sem("bwd_done"), sem("scaled_ready"), sem("den_ready"), sem("ln_ready"), sem("recip_ready"),
        sem("newton_ready"), sem("ratio_ready"))
    s_fold, s_vt = sem("fold_steps"), sem("vectors_transposed")
    s_sig1, s_r1, s_mm, s_z, s_gates = sem("sig1_ready"), sem("r1_ready"), sem("mm_done"), sem("z_ready"), sem("gates_ready")
    s_rec_steps, s_y, s_wo, s_x2, s_sig2, s_r2 = (
        sem("recurrence_steps"), sem("y_ready"), sem("wout_done"), sem("x2_ready"), sem("sig2_ready"), sem("r2_ready"))
    s_to, s_ev_x2, s_ev_r2, s_logit = sem("rows_transposed"), sem("x2_rows_ready"), sem("r2_rows_ready"), sem("logits_done")
    s_route, s_shift, s_pexp, s_sel, s_pos, s_dest, s_count = (
        sem("route_steps"), sem("shift_ready"), sem("prob_exp"), sem("sel_ready"), sem("pos_done"), sem("dest_ready"), sem("count_done"))

    N_V = 9
    N_VEC = N_V + 1
    ROUTE_STEPS = 17 + 2 * TT
    vec_cond = z_gate[:, 0, :]
    vec_rows = z_gate[0:N_V * CT, 1, 0:P]
    block = ctx.enter_context(nc.Block())

    def col(b, c, ct):
        return bass.ds(b * (2 * CT) + (c * CT + ct), 1)

    @block.sync
    def _(sp):
        def load_f(b):
            sp.dma_start(f_rows[:], fside[bass.ds(b, 1)].rearrange("o (i p) c -> p (o i) c", p=P)).then_inc(s_f_in, 16)

        def load_x(b):
            sp.dma_start(x_rows[:], x[bass.ds(b, 1)].rearrange("o (i p) c -> p (o i) c", p=P)).then_inc(s_x_in, 16)

        def store(b):
            sp.wait_ge(s_ev_x2, TT * (b + 1))
            sp.dma_start(out_rows[bass.ds(b * T, T)].rearrange("(i p) c -> p i c", p=P), x2_rows[:]).then_inc(s_x2_out, 16)

        load_f(0)
        load_x(0)
        sp.dma_start(vec_cond[:], cond.rearrange("b d -> (b d)").partition_broadcast(P)).then_inc(s_vec, 16)
        for n, v in ((W1C, w1c), (W2C, w2c), (U1C, u1c), (U2C, u2c), (BIN, b_in), (BGATE, b_gate),
                     (BOUT, b_out), (BDEC, b_decay), (DBIAS, decay_bias)):
            sp.dma_start(vec_rows[n * CT:(n + 1) * CT, :], v.rearrange("(t p) -> t p", p=P)).then_inc(s_vec, 16)
        for n, w in enumerate((W_in, W_decay, W_gate, W_out)):
            sp.dma_start(wm[:, n], w.rearrange("(t p) n -> p t n", p=P)).then_inc(s_w, 16)
        sp.dma_start(wg[:], Wg.rearrange("(t p) e -> p t e", p=P)).then_inc(s_w, 16)
        sp.wait_ge(s_template, 2)
        for n in range((NE + 1) * ST):
            sp.dma_start(slots[n * P:(n + 1) * P, :], r2_rows[:, 0, :]).then_inc(s_init, 16)
        with sp.Fori(1, B) as b:
            sp.wait_ge(s_f_tp, b * CT)
            load_f(b)
            sp.wait_ge(s_x_tp, b * CT)
            load_x(b)
        store(0)
        sp.wait_ge(s_f_tp, B * CT)
        load_f(B - 1)
        with sp.Fori(1, B) as b:
            store(b)
        sp.wait_ge(s_f_in, 16 * (B + 1))
        sp.wait_ge(s_x2_out, 16 * B)
        sp.wait_ge(s_init, 16 * (NE + 1) * ST)

    @block.gpsimd
    def _(pool):
        g = nc.gpsimd
        setup = Steps(pool, s_pool_setup, 0)
        setup.mark(g.memset(ident[:], 0.0))
        setup.mark(g.memset(lower[:], 1.0))
        setup.do(g.memset(ones[:], 1.0))
        setup.mark(g.affine_select(out=ident[:], in_=ident[:], compare_op=ALU.not_equal, fill=1.0, base=0,
                                   pattern=[[-1, P]], channel_multiplier=1))
        setup.mark(g.affine_select(out=lower[:], in_=lower[:], compare_op=ALU.is_gt, fill=0.0, base=0,
                                   pattern=[[1, P]], channel_multiplier=-1))
        setup.mark(g.iota(expert_no[:], [[0, TT], [1, NE]], base=0, channel_multiplier=0,
                          allow_small_or_imprecise_dtypes=True))
        setup.mark(g.iota(slot_base[:], [[0, TT], [CAP, NE]], base=0, channel_multiplier=0,
                          allow_small_or_imprecise_dtypes=True))
        setup.mark(g.iota(token_no[:], [[P, B * TT]], base=0, channel_multiplier=1))
        g.memset(carry[:], 0.0).then_inc(s_consts, 1)

        def products(u, ct):
            r = ct % 2
            pool.wait_ge(s_ek, u + 1)
            if not isinstance(u, int) or u >= 2:
                pool.wait_ge(s_den, u - 1)
            g.tensor_tensor(ekv[:, r], ek[:, r], kT[:, r], ALU.mult).then_inc(s_ekv, 1)
            pool.wait_ge(s_euk, u + 1)
            g.tensor_tensor(eukv[:, r, 0], euk[:, r, 0], kT[:, r], ALU.mult)
            g.tensor_tensor(eukv[:, r, 1], euk[:, r, 1], kT[:, r], ALU.mult).then_inc(s_eukv, 1)

        def newton(u, ct):
            r = ct % 2
            for c in range(2):
                pool.wait_ge(s_rec, 2 * u + c + 1)
                g.tensor_tensor(sums[:, r, c, 1], sums[:, r, c, 1], recip0[:, c], ALU.mult)
                g.tensor_tensor(sums[:, r, c, 0], sums[:, r, c, 0], recip0[:, c], ALU.mult).then_inc(s_newton, 1)

        def conditioning(b):
            for s in range(CT + 1):
                if s >= 1:
                    newton(b * CT + (s - 1), s - 1)
                if s < CT:
                    products(b * CT + (s + 1), (s + 1) % CT)

        def dispatch(b):
            pool.wait_ge(s_ev_r2, TT * (b + 1))
            pool.wait_ge(s_dest, b + 1)
            if first_batch(b):
                pool.wait_ge(s_init, 16 * (NE + 1) * ST)
            pool.nop(nofuse=True)
            for i in range(TT):
                for k in range(TOPK):
                    pool.indirect_dma_start(
                        out=slots, out_offset=bass.IndirectOffsetOnAxis(ap=dest[:, k, i:i + 1], axis=0),
                        in_=r2_rows[:, i, :], in_offset=None, bounds_check=NE * CAP - 1, oob_is_err=False,
                    ).then_inc(s_disp, 16)

        products(0, 0)
        conditioning(0)
        conditioning(1)
        with pool.Fori(2, B) as b:
            conditioning(b)
            dispatch(b - 2)
        dispatch(B - 2)
        dispatch(B - 1)
        pool.wait_ge(s_disp, 16 * TT * TOPK * B)

    @block.tensor
    def _(pe):
        def transpose_f(b, ct):
            u = b * CT + ct
            if ct == 0:
                pe.wait_ge(s_f_in, 16 * (b + 1))
            if not (isinstance(u, int) and u == 0):
                pe.wait_ge(s_k, u)
            for i in range(TT):
                last = nc.tensor.transpose(ps_f[:, i * P:(i + 1) * P], f_rows[:, i, ct * P:(ct + 1) * P], ident[:])
            last.then_inc(s_f_tp, 1)

        def transpose_x(b, ct):
            if ct == 0:
                pe.wait_ge(s_x_in, 16 * (b + 1))
                if at_least(b, 2):
                    pe.wait_ge(s_x2, CT * (b - 1))
            if not (first_batch(b) and ct == 0):
                pe.wait_ge(s_xT, b * CT + ct)
            for i in range(TT):
                last = nc.tensor.transpose(ps_x[:, i * P:(i + 1) * P], x_rows[:, i, ct * P:(ct + 1) * P], ident[:])
            last.then_inc(s_x_tp, 1)

        def gate(b, k):
            m, e = GATE_TILES[k]
            if k == 0:
                pe.wait_ge(s_r1, b + 1)
                if at_least(b, 1):
                    pe.wait_ge(s_x2, CT * b)
            if k >= 3:
                pe.wait_ge(s_z, Z_COPIES * b + k - 2)
            for dt in range(CT):
                last = nc.tensor.matmul(ps_mm[:, k % 3, :], wm[:, m, dt, e * P:(e + 1) * P],
                                        r1T[:, bass.ds(b % 2, 1), dt, :].rearrange("p o t -> p (o t)"),
                                        start=(dt == 0), stop=(dt == CT - 1))
            last.then_inc(s_mm, 1)

        def project(b, x_done):
            for dt in range(CT):
                pe.wait_ge(s_y, CT * b + dt + 1)
                for e in range(CT):
                    if dt == 0 and e == 1:
                        pe.wait_ge(s_xT, CT * x_done)
                    if dt == 0 and e == 2:
                        pe.wait_ge(s_gates, CT * (b + 1))
                    last = nc.tensor.matmul(bank(e), wm[:, 3, dt, e * P:(e + 1) * P], z_gate[:, dt, :],
                                            start=(dt == 0), stop=(dt == CT - 1))
                    if dt == CT - 1:
                        last.then_inc(s_wo, 1)

        def x2_row(b, i):
            if i == 0:
                pe.wait_ge(s_x2, CT * (b + 1))
                if at_least(b, 1):
                    pe.wait_ge(s_ev_r2, TT * b)
            else:
                pe.wait_ge(s_ev_x2, TT * b + i)
            for ct in range(CT):
                last = nc.tensor.transpose(ps_to[:, ct * P:(ct + 1) * P], z_dec[:, ct, i * P:(i + 1) * P], ident[:])
            last.then_inc(s_to, 1)

        def r2_row(b, i):
            if i == 0:
                pe.wait_ge(s_r2, b + 1)
                pe.wait_ge(s_ev_x2, TT * (b + 1))
            else:
                pe.wait_ge(s_ev_r2, TT * b + i)
            for ct in range(CT):
                last = nc.tensor.transpose(ps_to[:, ct * P:(ct + 1) * P], sig[:, ct, i * P:(i + 1) * P], ident[:])
            last.then_inc(s_to, 1)

        def logits(b):
            pe.wait_ge(s_r2, b + 1)
            if at_least(b, 1):
                pe.wait_ge(s_dest, b)
            for i in range(TT):
                for ct in range(CT):
                    last = nc.tensor.matmul(ps_logit[:, i, :], sig[:, ct, i * P:(i + 1) * P], wg[:, ct, :],
                                            start=(ct == 0), stop=(ct == CT - 1))
            last.then_inc(s_logit, 1)

        def places(b):
            pe.wait_ge(s_sel, b + 1)
            for i in range(TT):
                nc.tensor.matmul(ps_pos[:, i, :], lower[:], sel[:, i, :], start=True, stop=False)
                for j in range(i):
                    nc.tensor.matmul(ps_pos[:, i, :], ones[:], sel[:, j, :], start=False, stop=False)
                last = nc.tensor.matmul(ps_pos[:, i, :], ones[:], carry[:], start=False, stop=True)
            last.then_inc(s_pos, 1)

        def step(b, cond, gates, tail):
            if cond:
                transpose_f(b, 1)
            if tail:
                project(b - 2, b if cond else B)
            if cond:
                transpose_f(b, 2)
            for k in range(len(GATE_TILES)):
                if gates:
                    gate(b - 1, k)
                if tail and k < TT:
                    x2_row(b - 2, k)
                if tail and k == 5:
                    logits(b - 2)
                if tail and 5 <= k <= 8:
                    r2_row(b - 2, k - 5)
                if cond and k == 2:
                    transpose_f(b, 3)
                if cond and k == 5:
                    transpose_f(b + 1, 0)
                if cond and 6 <= k <= 9:
                    transpose_x(b, k - 6)
                if tail and k == 9:
                    places(b - 2)

        pe.wait_ge(s_pool_setup, 8)
        pe.wait_ge(s_vec, 16 * N_VEC)
        nc.tensor.transpose(ps_small[:, 0:N_V * CT], vec_rows, ident[0:N_V * CT, 0:N_V * CT]).then_inc(s_vt, 1)

        pe.wait_ge(s_consts, 2)
        transpose_f(0, 0)
        step(0, True, False, False)
        pe.wait_ge(s_w, 16 * 5)
        step(1, True, True, False)
        with pe.Fori(2, B) as b:
            step(b, True, True, True)
        step(B, False, True, True)
        step(B + 1, False, False, True)
        pe.wait_ge(s_dest, B)
        nc.tensor.matmul(ps_count, ones[:], carry[:], start=True, stop=True).then_inc(s_count, 1)

    @block.scalar
    def _(act):
        a = nc.scalar

        def copy_f(b, ct):
            u = b * CT + ct
            act.wait_ge(s_f_tp, u + 1)
            if at_least(u, 2):
                act.wait_ge(s_eukv, u - 1)
            a.activation(kT[:, ct % 2], ps_f[:], ACT.Copy).then_inc(s_k, 1)

        def copy_x(b, ct):
            act.wait_ge(s_x_tp, b * CT + ct + 1)
            if ct == 0 and at_least(b, 2):
                act.wait_ge(s_x2, CT * (b - 1))
            act.nop(nofuse=True)
            a.activation(xT[:, bass.ds(b % 2, 1), ct, :], ps_x[:].rearrange("p (o t) -> p o t", o=1),
                         ACT.Copy).then_inc(s_xT, 1)

        def exps(b, ct):
            u, r = b * CT + ct, ct % 2
            act.wait_ge(s_caps, u + 1)
            a.activation(ek[:, r], ek[:, r], ACT.Exp).then_inc(s_ek, 1)
            a.activation(euk[:, r], euk[:, r], ACT.Exp).then_inc(s_euk, 1)

        def scale(b, ct):
            u, r = b * CT + ct, ct % 2
            if at_least(u, 1):
                act.wait_ge(s_den, u)
            for c in range(2):
                act.wait_ge(s_bwd, 2 * u + c + 1)
                a.activation(scaled[:, c, :, 1:T], sums[:, r, c, :, 1:T], ACT.Copy,
                             scale=one_md2[:, col(b, c, ct)]).then_inc(s_scaled, 1)

        def first_reciprocal(b, ct):
            u, r = b * CT + ct, ct % 2
            act.wait_ge(s_den, u + 1)
            if not isinstance(b, int) or u >= 1:
                act.wait_ge(s_newton, 2 * u)
            for c in range(2):
                a.activation(recip0[:, c], sums[:, r, c, 1], ACT.Ln).then_inc(s_ln, 1)
            for c in range(2):
                act.wait_ge(s_ln, 2 * u + c + 1)
                a.activation(recip0[:, c], recip0[:, c], ACT.Exp, scale=-1.0).then_inc(s_rec, 1)

        def gate_source(k):
            m, e = GATE_TILES[k]
            return (z_in, z_dec, z_gate)[m], (vec[:, BIN, e:e + 1], bdec[:, e:e + 1], vec[:, BGATE, e:e + 1])[m], e

        def gate_sum(b, k):
            if k == 0 and at_least(b, 1):
                act.wait_ge(s_wo, CT * b)
            if k == CT and at_least(b, 1):
                act.wait_ge(s_to, 2 * TT * (b - 1) + TT)
            z, bias, e = gate_source(k)
            act.wait_ge(s_mm, 12 * b + k + 1)
            a.activation(z[:, e], ps_mm[:, k % 3, :], ACT.Identity, bias=bias).then_inc(s_z, 1)

        def gate_functions(b):
            act.wait_ge(s_z, Z_COPIES * b + CT)
            a.activation(z_in[:], z_in[:], ACT.Silu)
            act.wait_ge(s_z, Z_COPIES * (b + 1))
            for k in range(CT, len(GATE_TILES)):
                z, bias, e = gate_source(k)
                if k < Z_COPIES:
                    last = a.activation(z[:, e], z[:, e], ACT.Sigmoid)
                else:
                    act.wait_ge(s_mm, 12 * b + k + 1)
                    last = a.activation(z[:, e], ps_mm[:, k % 3, :], ACT.Sigmoid, bias=bias)
                if GATE_TILES[k][0] == 2:
                    last.then_inc(s_gates, 1)

        def sigmoid_x(b):
            act.wait_ge(s_xT, CT * (b + 1))
            if at_least(b, 1):
                act.wait_ge(s_r1, b)
            if at_least(b, 2):
                act.wait_ge(s_to, 2 * TT * (b - 1))
            act.nop(nofuse=True)
            a.activation(sig[:], xT[:, bass.ds(b % 2, 1)].rearrange("p o c t -> p (o c) t"), ACT.Sigmoid).then_inc(s_sig1, 1)

        def sigmoid_x2(b, r1_done):
            act.wait_ge(s_x2, CT * (b + 1))
            act.wait_ge(s_r1, r1_done)
            if at_least(b, 1):
                act.wait_ge(s_to, 2 * TT * b)
            a.activation(sig[:], z_dec[:], ACT.Sigmoid).then_inc(s_sig2, 1)

        def x2_row(b, i):
            if i == 0 and at_least(b, 1):
                act.wait_ge(s_x2_out, 16 * b)
            act.wait_ge(s_to, 2 * TT * b + i + 1)
            a.activation(x2_rows[:, i], ps_to[:], ACT.Copy).then_inc(s_ev_x2, 1)

        def r2_row(b, i):
            if i == 0 and first_batch(b):
                act.wait_ge(s_init, 16 * (NE + 1) * ST)
            elif i == 0:
                act.wait_ge(s_disp, 16 * TT * TOPK * b)
            act.wait_ge(s_to, 2 * TT * b + TT + i + 1)
            a.activation(r2_rows[:, i, 0:C], ps_to[:], ACT.Copy).then_inc(s_ev_r2, 1)

        def probabilities(b):
            act.wait_ge(s_shift, b + 1)
            a.activation(pe_[:], pe_[:], ACT.Exp).then_inc(s_pexp, 1)

        def step(b, cond, gates, tail):
            def sums_of(ks):
                if gates:
                    for k in ks:
                        gate_sum(b - 1, k)

            def unit(s):
                if cond:
                    copy_f(b if s + 1 < CT else b + 1, (s + 1) % CT)
                    if s >= 1:
                        first_reciprocal(b, s - 1)
                    scale(b, s)
                    exps(b if s + 1 < CT else b + 1, (s + 1) % CT)

            if cond:
                act.preload_act_table_set("natural_log_exp_and_others")
            unit(0)
            unit(1)
            if tail:
                sigmoid_x2(b - 2, b if cond else B)
                act.preload_act_table_set("natural_log_exp_and_others")
            for k in (0, 1, 2):
                sums_of([k])
                if tail:
                    x2_row(b - 2, k)
            unit(2)
            for k in (3, 4, 5, 6):
                sums_of([k])
                if tail and k == 3:
                    x2_row(b - 2, k)
                if tail and k >= 5:
                    r2_row(b - 2, k - 5)
            if cond:
                copy_x(b, 0)
            unit(3)
            for k in (7, 8, 9):
                sums_of([k])
                if tail and k <= 8:
                    r2_row(b - 2, k - 5)
                if cond:
                    copy_x(b, k - 6)
            if tail:
                probabilities(b - 2)
            if cond:
                first_reciprocal(b, CT - 1)
            if gates:
                gate_functions(b - 1)
            if cond:
                sigmoid_x(b)

        act.wait_ge(s_setup_v, 1)
        setup = Steps(act, s_setup_a, 0)
        setup.do(a.activation(ew[:], vec[:, W1C:W2C + 1, :], ACT.Exp))
        setup.do(a.activation(ew[:], ew[:], ACT.Exp, scale=-1.0))
        act.wait_ge(s_setup_v, 2)
        setup.do(a.activation(tf[:], tf[:], ACT.Sigmoid))
        act.wait_ge(s_consts, 2)
        copy_f(0, 0)
        exps(0, 0)
        step(0, True, False, False)
        step(1, True, True, False)
        with act.Fori(2, B) as b:
            step(b, True, True, True)
        step(B, False, True, True)
        step(B + 1, False, False, True)

    @block.vector
    def _(dve):
        v = nc.vector
        d0 = lambda b, c, ct, n: ps_decay[:, col(b, c, ct)].to_broadcast([P, n])

        setup = Steps(dve, s_setup_v, 0)
        dve.wait_ge(s_vt, 1)
        setup.do(v.tensor_copy(vec[:].rearrange("p n t -> p (n t)"), ps_small[:, 0:N_V * CT]))
        dve.wait_ge(s_vec, 16 * N_VEC)
        setup.mark(v.tensor_reduce(tf[:], vec_cond.rearrange("p (b d) -> p b d", b=B), AX.X, ALU.add))
        setup.mark(v.tensor_tensor(bdec[:], vec[:, BDEC], vec[:, DBIAS], ALU.add))
        dve.wait_ge(s_setup_a, 3)
        setup.mark(v.tensor_scalar(half_tf[:], tf[:], 0.5, 0.5, ALU.mult, ALU.add))
        setup.mark(v.tensor_scalar(neg_scale[:], tf[:], 0.2, 0.8, ALU.mult, ALU.add))
        setup.wait()
        setup.mark(v.tensor_scalar(neg_scale[:], neg_scale[:], -1.0, None, ALU.mult))
        for b in range(B):
            setup.mark(v.tensor_scalar(decay[:, b * 2 * CT:(b + 1) * 2 * CT], ew[:].rearrange("p c t -> p (c t)"),
                                       half_tf[:, b:b + 1], None, ALU.mult))
        setup.wait()
        setup.mark(v.tensor_copy(ps_decay, decay[:]))
        setup.mark(v.tensor_scalar(one_m[:], decay[:], -1.0, 1.0, ALU.mult, ALU.add))
        setup.wait()
        v.scalar_tensor_tensor(out=one_md2[:], in0=decay[:], scalar=1.0, in1=one_m[:], op0=ALU.add,
                               op1=ALU.mult).then_inc(s_consts, 1)
        v.memset(r2_rows[:], 0.0).then_inc(s_template, 1)
        dve.wait_ge(s_template, 1)
        v.memset(r2_rows[:, 0, C + NE:ROW].bitcast(U32), NO_TOKEN).then_inc(s_template, 1)

        def caps(b, ct):
            u, r = b * CT + ct, ct % 2
            dve.wait_ge(s_k, u + 1)
            if at_least(u, 2):
                dve.wait_ge(s_den, u - 1)
            v.tensor_scalar(ek[:, r], kT[:, r], CAPV, None, ALU.min)
            for c in range(2):
                last = v.tensor_scalar(euk[:, r, c], kT[:, r], vec[:, U1C + c, ct:ct + 1], CAPV, ALU.add, ALU.min)
            last.then_inc(s_caps, 1)

        def backward(b, ct):
            u, r = b * CT + ct, ct % 2
            dve.wait_ge(s_ekv, u + 1)
            if at_least(u, 2):
                dve.wait_ge(s_ratio, u - 1)
            for c in range(2):
                v.tensor_tensor_scan(sums[:, r, c, 1, ::-1], d0(b, c, ct, T), ek[:, r, ::-1], 0.0, ALU.mult, ALU.add)
                v.tensor_tensor_scan(sums[:, r, c, 0, ::-1], d0(b, c, ct, T), ekv[:, r, ::-1], 0.0, ALU.mult, ALU.add).then_inc(s_bwd, 1)

        def fold(b, ct):
            u, r = b * CT + ct, ct % 2
            steps = Steps(dve, s_fold, 6 * u)
            for c in range(2):
                dve.wait_ge(s_scaled, 2 * u + c + 1)
                for n in range(2):
                    s = sums[:, r, c, n]
                    ins = v.tensor_tensor_scan(s[:, 1:T], d0(b, c, ct, T - 1), scaled[:, c, n, 1:T], s[:, 0:1], ALU.mult, ALU.add)
                    if n == 1:
                        steps.mark(ins)
            steps.wait()
            steps.mark(v.tensor_tensor(sums[:, r, 0, 1], sums[:, r, 0, 1], euk[:, r, 0], ALU.add))
            steps.mark(v.tensor_tensor(sums[:, r, 1, 1], sums[:, r, 1, 1], euk[:, r, 1], ALU.add))
            dve.wait_ge(s_eukv, u + 1)
            steps.mark(v.tensor_tensor(sums[:, r, 0, 0], sums[:, r, 0, 0], eukv[:, r, 0], ALU.add))
            steps.do(v.tensor_tensor(sums[:, r, 1, 0], sums[:, r, 1, 0], eukv[:, r, 1], ALU.add))
            v.tensor_scalar(sums[:, r, :, 1], sums[:, r, :, 1], DEN_MIN, None, ALU.max).then_inc(s_den, 1)

        def ratio(b, ct):
            u, r = b * CT + ct, ct % 2
            for c, dst in enumerate((r1T, ratio2)):
                dve.wait_ge(s_newton, 2 * u + c + 1)
                if ct == 0 and at_least(b, 2):
                    dve.wait_ge(*((s_mm, 12 * (b - 1)) if c == 0 else (s_r2, b - 1)))
                last = v.scalar_tensor_tensor(out=dst[:, bass.ds(b % 2, 1), ct, :],
                                              in0=sums[:, r, c, 1].rearrange("p (o t) -> p o t", o=1), scalar=2.0,
                                              in1=sums[:, r, c, 0].rearrange("p (o t) -> p o t", o=1),
                                              op0=ALU.subtract, op1=ALU.mult)
            last.then_inc(s_ratio, 1)

        def first_out(b):
            dve.wait_ge(s_sig1, b + 1)
            dve.wait_ge(s_ratio, CT * (b + 1))
            r1 = r1T[:, bass.ds(b % 2, 1)].rearrange("p o c t -> p (o c) t")
            v.scalar_tensor_tensor(out=r1, in0=r1, scalar=neg_scale[:, bass.ds(b, 1)], in1=sig[:],
                                   op0=ALU.mult, op1=ALU.mult).then_inc(s_r1, 1)

        def recurrence(b):
            steps = Steps(dve, s_rec_steps, 2 * CT * b)
            for e in range(CT):
                dve.wait_ge(s_gates, CT * b + e + 1)
                steps.do(v.scalar_tensor_tensor(out=z_in[:, e], in0=z_dec[:, e], scalar=1.0, in1=z_in[:, e],
                                                op0=ALU.subtract, op1=ALU.mult))
                steps.do(v.tensor_tensor_scan(z_in[:, e], z_dec[:, e], z_in[:, e], 0.0, ALU.mult, ALU.subtract))
                v.tensor_tensor(z_gate[:, e], z_gate[:, e], z_in[:, e], ALU.mult).then_inc(s_y, 1)

        def residual(b):
            for e in range(CT):
                dve.wait_ge(s_wo, CT * b + e + 1)
                if e == 0:
                    dve.wait_ge(s_y, CT * (b + 1))
                v.scalar_tensor_tensor(out=z_dec[:, e:e + 1], in0=bank(e).rearrange("p (o t) -> p o t", o=1), scalar=vec[:, BOUT, e:e + 1],
                                       in1=xT[:, bass.ds(b % 2, 1), e, :], op0=ALU.add, op1=ALU.add).then_inc(s_x2, 1)

        def second_out(b):
            dve.wait_ge(s_sig2, b + 1)
            v.scalar_tensor_tensor(out=sig[:], in0=ratio2[:, bass.ds(b % 2, 1)].rearrange("p o c t -> p (o c) t"),
                                   scalar=neg_scale[:, bass.ds(b, 1)], in1=sig[:],
                                   op0=ALU.mult, op1=ALU.mult).then_inc(s_r2, 1)

        bc = lambda ap: ap.to_broadcast([P, TT, NE])

        def select(b, st):
            dve.wait_ge(s_logit, b + 1)
            st.do(v.tensor_copy(logit[:], ps_logit))
            dve.nop(nofuse=True)
            for i in range(TT):
                st.mark(v.max(top[:, i], logit[:, i]))
            st.wait()
            v.tensor_tensor(pe_[:], logit[:], bc(top[:, :, 0:1]), ALU.subtract).then_inc(s_shift, 1)
            for i in range(TT):
                st.mark(v.max_index(top_i[:, i], top[:, i], logit[:, i]))
            st.wait()
            st.do(v.tensor_copy(top_f[:], top_i[:]))
            for k in range(TOPK):
                st.mark(v.tensor_tensor(oh[:, k], expert_no[:], bc(top_f[:, :, k:k + 1]), ALU.is_equal))
            st.wait()
            v.tensor_tensor(sel[:], oh[:, 0], oh[:, 1], ALU.add).then_inc(s_sel, 1)
            dve.wait_ge(s_sel, b + 1)
            st.mark(v.tensor_reduce(sel_sum[:], sel[:].rearrange("p i e -> p e i"), AX.X, ALU.add))

        def place(b, st):
            dve.wait_ge(s_ev_r2, TT * (b + 1))
            st.mark(v.tensor_copy(r2_rows[:, :, C + NE:ROW].bitcast(U32),
                                  token_no[:, bass.ds(b * TT, TT)].rearrange("p (i o) -> p i o", o=1)))
            dve.wait_ge(s_pexp, b + 1)
            st.do(v.tensor_reduce(psum_[:], pe_[:], AX.X, ALU.add))
            st.do(v.reciprocal(psum_[:], psum_[:]))
            st.mark(v.tensor_tensor(r2_rows[:, :, C:C + NE], pe_[:], bc(psum_[:].rearrange("p (i o) -> p i o", o=1)), ALU.mult))
            dve.wait_ge(s_pos, b + 1)
            st.do(v.tensor_scalar(slot_t[:], ps_pos, float(CAP), float(NO_TOKEN), ALU.is_ge, ALU.mult))
            st.do(v.tensor_tensor(slot_f[:], ps_pos, slot_t[:], ALU.add))
            st.do(v.tensor_tensor(slot_f[:], slot_f[:], slot_base[:], ALU.add))
            for k in range(TOPK):
                st.do(v.tensor_tensor(slot_t[:], slot_f[:], oh[:, k], ALU.mult))
                st.do(v.tensor_reduce(dest_f[:, k], slot_t[:], AX.X, ALU.add))
            st.do(v.tensor_tensor(carry[:], carry[:], sel_sum[:], ALU.add))
            if not (first_batch(b)):
                dve.wait_ge(s_disp, 16 * TT * TOPK * b)
            v.tensor_copy(dest[:], dest_f[:]).then_inc(s_dest, 1)
            assert st.n == ROUTE_STEPS, st.n

        dve.wait_ge(s_consts, 2)
        dve.wait_ge(s_pool_setup, 8)
        def step(b, cond, gates, tail):
            st = Steps(dve, s_route, ROUTE_STEPS * (b - 2)) if tail else None
            for s in range(CT):
                if cond:
                    backward(b, s)
                    caps(b if s + 1 < CT else b + 1, (s + 1) % CT)
                if tail and s == 1:
                    residual(b - 2)
                if cond:
                    fold(b, s)
                if tail and s == 1:
                    second_out(b - 2)
                if tail and s == 2:
                    select(b - 2, st)
                if cond and s >= 1:
                    ratio(b, s - 1)
            if cond:
                ratio(b, CT - 1)
            if gates:
                recurrence(b - 1)
            if cond:
                first_out(b)
            if tail:
                place(b - 2, st)

        caps(0, 0)
        step(0, True, False, False)
        step(1, True, True, False)
        with dve.Fori(2, B) as b:
            step(b, True, True, True)
        step(B, False, True, True)
        step(B + 1, False, False, True)
        dve.wait_ge(s_count, 1)
        v.tensor_copy(counts[:], ps_count).then_inc(s_count, 1)
        dve.wait_ge(s_count, 2)


def experts(nc, ctx, ident, counts, slots, out_rows, w1, w2):
    def sb(name, shape, dt=F32):
        return ctx.enter_context(nc.sbuf_tensor(name, shape, dt))

    def ps(name, shape, dt=F32):
        return ctx.enter_context(nc.psum_tensor(name, shape, dt))

    def sem(name):
        return ctx.enter_context(nc.semaphore(name))

    FW = FC * P
    raw1 = sb("raw1", [P, 2, CT, FW])
    raw2 = sb("raw2", [P, 2, FC, C])
    w1h, w1l = sb("w1h", [P, 2, CT, FW], F32R), sb("w1l", [P, 2, CT, FW], F32R)
    w2h, w2l = sb("w2h", [P, 2, FC, C], F32R), sb("w2l", [P, 2, FC, C], F32R)
    rows = sb("rows", [P, ST, ROW])
    xh, xl = sb("xh", [P, 2, CT, CAP], F32R), sb("xl", [P, 2, CT, CAP], F32R)
    hh, hl = sb("hh", [P, 2, CAP], F32R), sb("hl", [P, 2, CAP], F32R)
    y = sb("y", [P, ST, C])
    gate = sb("gate", [P, ST])
    token = sb("token", [P, ST], U32)

    ps_y = ps("ps_y", [P, ST, C])
    ps_h = ps("ps_h", [P, 2, 512])
    ps_t = ps("ps_t", [P, CT, P])

    s_w, s_rows = [sem("weights_in_even"), sem("weights_in_odd")], sem("rows_in")
    s_wh, s_wl = sem("weights_high"), sem("weights_low")
    s_tp, s_xh, s_xl = sem("rows_transposed2"), sem("x_high"), sem("x_low")
    s_h, s_hh, s_hl, s_f = sem("hidden_done"), sem("hidden_high"), sem("hidden_low"), sem("hidden_used")
    s_y, s_ya, s_yv = sem("y_done"), sem("y_even"), sem("y_odd")
    s_gate, s_token, s_add = sem("gate_ready"), sem("token_ready"), sem("rows_added")
    s_y0 = sem("y_cleared")

    SPLIT_AT = {0: range(0, 0), 1: range(0, 3), 2: range(3, 7), 3: range(7, 8)}
    TURN_AT = {3: 0, 5: 1, 7: 2, 9: 3, 11: 4}
    CLASSES = (3, 4, 5)

    def piece(n, high, low, ring):
        if n < CT:
            return high[0][:, ring, n], low[0][:, ring, n], raw1[:, ring, n]
        return high[1][:, ring, n - CT], low[1][:, ring, n - CT], raw2[:, ring, n - CT]

    def by_class(eng, e, body):
        n = eng.value_load(counts[0:1, bass.ds(e, 1)], min_val=0, max_val=B * T)
        with eng.If(n < CLASSES[0] * P + 1):
            body(CLASSES[0])
        with eng.Else():
            with eng.If(n < CLASSES[1] * P + 1):
                body(CLASSES[1])
            with eng.Else():
                body(CLASSES[2])

    block = ctx.enter_context(nc.Block())

    @block.sync
    def _(sp):
        def weights(e, c):
            sp.dma_start(raw1[:, c % 2], w1[bass.ds(e, 1), :, c * FW:(c + 1) * FW].rearrange("o (t p) f -> p (o t) f", p=P)).then_inc(s_w[c % 2], 16)
            sp.dma_start(raw2[:, c % 2], w2[bass.ds(e, 1), c * FW:(c + 1) * FW, :].rearrange("o (t p) n -> p (o t) n", p=P)).then_inc(s_w[c % 2], 16)

        def load_rows(e):
            sp.dma_start(rows[:], slots[bass.ds(e * CAP, CAP)].rearrange("(i p) c -> p i c", p=P)).then_inc(s_rows, 16)

        def expert(e):
            for c in range(NC):
                if not (isinstance(e, int) and c < 2):
                    sp.wait_ge(s_wl, PIECES * (e * NC + (c - 1)))
                weights(e, c)
                if c == 1:
                    sp.wait_ge(s_tp, ST * (e + 1))
                    sp.wait_ge(s_gate, e + 1)
                    sp.wait_ge(s_token, e + 1)
                    load_rows(e + 1)

        load_rows(0)
        expert(0)
        with sp.Fori(1, NE) as e:
            expert(e)
        sp.wait_ge(s_wl, PIECES * (NE * NC - 1))
        weights(0, 0)
        sp.wait_ge(s_w[0], 32 * (NE * NC // 2 + 1))
        sp.wait_ge(s_w[1], 32 * (NE * NC // 2))
        sp.wait_ge(s_rows, 16 * (NE + 1))

    @block.gpsimd
    def _(pool):
        nc.gpsimd.memset(y[:], 0.0).then_inc(s_y0, 1)
        def expert(e, first):
            pool.wait_ge(s_rows, 16 * (e + 1))
            if not first:
                pool.wait_ge(s_add, 16 * ST * e)
            pool.nop(nofuse=True)
            nc.gpsimd.tensor_copy(token[:], rows[:, :, C + NE:ROW].bitcast(U32).rearrange("p i o -> p (i o)")).then_inc(s_token, 1)
            pool.wait_ge(s_token, e + 1)
            pool.wait_ge(s_ya, e + 2)
            pool.wait_ge(s_yv, e + 2)
            pool.wait_ge(s_y0, 1)
            pool.nop(nofuse=True)
            for i in range(ST):
                pool.indirect_dma_start(
                    out=out_rows, out_offset=bass.IndirectOffsetOnAxis(ap=token[:, i:i + 1], axis=0),
                    in_=y[:, i, :], in_offset=None, bounds_check=B * T - 1, oob_is_err=False,
                    compute_op=ALU.add).then_inc(s_add, 16)
        expert(0, True)
        with pool.Fori(1, NE) as e:
            expert(e, False)
        pool.wait_ge(s_add, 16 * ST * NE)

    @block.tensor
    def _(pe):
        def turn(e, i):
            pe.wait_ge(s_rows, 16 * (e + 1))
            if not (isinstance(e, int) and i == 0):
                pe.wait_ge(s_xl, ST * e + i)
            for ct in range(CT):
                last = nc.tensor.transpose(ps_t[:, ct, :], rows[:, i, ct * P:(ct + 1) * P], ident[:])
            last.then_inc(s_tp, 1)

        def up(e, par, f, t):
            g = e * NC + f // FC
            if f % FC == 0:
                pe.wait_ge(s_wl, PIECES * (g + 1))
            if f == 0:
                pe.wait_ge(s_xl, ST * (e + 1))
            hidden = e * FT + f
            pe.wait_ge(s_hl, hidden + 1)
            r, j = (f // FC) % 2, f % FC
            parts = ((0, t * P // 2), (t * P // 2, t * P)) if t * P > 512 else ((0, t * P),)
            for n, (lo, hi) in enumerate(parts):
                for dt in range(CT):
                    wcol = slice(j * P, (j + 1) * P)
                    o = ps_h[:, n, 0:hi - lo]
                    nc.tensor.matmul(o, w1h[:, r, dt, wcol], xh[:, par, dt, lo:hi], start=(dt == 0), stop=False)
                    nc.tensor.matmul(o, w1h[:, r, dt, wcol], xl[:, par, dt, lo:hi], start=False, stop=False)
                    last = nc.tensor.matmul(o, w1l[:, r, dt, wcol], xh[:, par, dt, lo:hi], start=False, stop=(dt == CT - 1))
            last.then_inc(s_h, 1)

        def down(e, f, t):
            if f == 0:
                pe.wait_ge(s_ya, e + 1)
                pe.wait_ge(s_yv, e + 1)
            pe.wait_ge(s_hl, e * FT + f + 2)
            r, j = (f // FC) % 2, f % FC
            for i in range(t):
                tok = slice(i * P, (i + 1) * P)
                nc.tensor.matmul(ps_y[:, i, :], hh[:, f % 2, tok], w2h[:, r, j], start=(f == 0), stop=False)
                nc.tensor.matmul(ps_y[:, i, :], hl[:, f % 2, tok], w2h[:, r, j], start=False, stop=False)
                last = nc.tensor.matmul(ps_y[:, i, :], hh[:, f % 2, tok], w2l[:, r, j], start=False, stop=(f == FT - 1))
            last.then_inc(s_y if f == FT - 1 else s_f, 1)

        for i in range(ST):
            turn(0, i)
        with pe.Fori(0, NE // 2) as pair:
            for par in range(2):
                e = pair * 2 + par

                def body(t):
                    up(e, par, 0, t)
                    for f in range(FT):
                        if f + 1 < FT:
                            up(e, par, f + 1, t)
                        if f in TURN_AT:
                            turn(e + 1, TURN_AT[f])
                        down(e, f, t)
                by_class(pe, e, body)

    @block.scalar
    def _(act):
        a = nc.scalar

        def token_high(e, par, i):
            act.wait_ge(s_tp, ST * e + i + 1)
            a.activation(xh[:, par, :, i * P:(i + 1) * P], ps_t[:], ACT.Copy).then_inc(s_xh, 1)

        def weight_high(e, c, n):
            ring = c % 2
            if n == 0:
                act.wait_ge(s_w[ring], 32 * (e * (NC // 2) + (c // 2 + 1)))
            h, _, raw = piece(n, (w1h, w2h), (w1l, w2l), ring)
            a.activation(h, raw, ACT.Copy).then_inc(s_wh, 1)

        act.sem_inc(s_ya, 1)
        for n in range(PIECES):
            weight_high(0, 0, n)
        for i in range(ST):
            token_high(0, 0, i)
        with act.Fori(0, NE // 2) as pair:
            for par in range(2):
                e = pair * 2 + par

                def body(t):
                    for f in range(FT):
                        hidden = e * FT + f
                        act.wait_ge(s_h, hidden + 1)
                        if f >= 2:
                            act.wait_ge(s_f, e * (FT - 1) + (f - 1))
                        half = t * P // 2
                        if t * P > 512:
                            a.activation(hh[:, f % 2, 0:t * P].rearrange("p (n s) -> p n s", n=2), ps_h[:, :, 0:half], ACT.Relu).then_inc(s_hh, 1)
                        else:
                            a.activation(hh[:, f % 2, 0:t * P], ps_h[:, 0, 0:t * P], ACT.Relu).then_inc(s_hh, 1)
                        c = f // FC
                        for n in SPLIT_AT[f % FC]:
                            if n == 0 and c > 0:
                                act.wait_ge(s_f, e * (FT - 1) + c * FC)
                            weight_high(e, c + 1, n)
                        if f in TURN_AT:
                            token_high(e + 1, 1 - par, TURN_AT[f])
                    act.wait_ge(s_y, e + 1)
                    act.wait_ge(s_gate, e + 1)
                    act.wait_ge(s_y0, 1)
                    act.wait_ge(s_token, e + 1)
                    for i in range(0, t, 2):
                        last = a.activation(y[:, i], ps_y[:, i, :], ACT.Copy, scale=gate[:, i:i + 1])
                    last.then_inc(s_ya, 1)
                by_class(act, e, body)

    @block.vector
    def _(dve):
        v = nc.vector

        def token_low(e, par, i):
            dve.wait_ge(s_xh, ST * e + i + 1)
            s = slice(i * P, (i + 1) * P)
            v.tensor_tensor(xl[:, par, :, s], ps_t[:], xh[:, par, :, s].bitcast(F32), ALU.subtract).then_inc(s_xl, 1)

        def weight_low(g, ring, n):
            dve.wait_ge(s_wh, PIECES * g + n + 1)
            h, l, raw = piece(n, (w1h, w2h), (w1l, w2l), ring)
            v.tensor_tensor(l, raw, h.bitcast(F32), ALU.subtract).then_inc(s_wl, 1)

        dve.sem_inc(s_hl, 1)
        dve.sem_inc(s_yv, 1)
        for n in range(PIECES):
            weight_low(0, 0, n)
        for i in range(ST):
            token_low(0, 0, i)
        with dve.Fori(0, NE // 2) as pair:
            for par in range(2):
                e = pair * 2 + par
                dve.wait_ge(s_rows, 16 * (e + 1))
                dve.wait_ge(s_ya, e + 1)
                dve.wait_ge(s_yv, e + 1)
                v.tensor_copy(gate[:], rows[:, :, bass.ds(e + C, 1)].rearrange("p i o -> p (i o)")).then_inc(s_gate, 1)

                def body(t):
                    for f in range(FT):
                        dve.wait_ge(s_hh, e * FT + f + 1)
                        half = t * P // 2
                        if t * P > 512:
                            o, src, high = (z.rearrange("p (n s) -> p n s", n=2) if k else z for k, z in
                                            ((1, hl[:, f % 2, 0:t * P]), (0, ps_h[:, :, 0:half]), (1, hh[:, f % 2, 0:t * P].bitcast(F32))))
                        else:
                            o, src, high = hl[:, f % 2, 0:t * P], ps_h[:, 0, 0:t * P], hh[:, f % 2, 0:t * P].bitcast(F32)
                        v.scalar_tensor_tensor(out=o, in0=src, scalar=0.0, in1=high, op0=ALU.max, op1=ALU.subtract).then_inc(s_hl, 1)
                        c = f // FC
                        for n in SPLIT_AT[f % FC]:
                            weight_low(e * NC + (c + 1), (c + 1) % 2, n)
                        if f in TURN_AT:
                            token_low(e + 1, 1 - par, TURN_AT[f])
                    dve.wait_ge(s_y, e + 1)
                    dve.wait_ge(s_gate, e + 1)
                    dve.wait_ge(s_y0, 1)
                    dve.wait_ge(s_token, e + 1)
                    for i in range(1, t, 2):
                        last = v.tensor_scalar(y[:, i], ps_y[:, i, :], gate[:, i:i + 1], None, ALU.mult)
                    last.then_inc(s_yv, 1)
                by_class(dve, e, body)


_INS = ["x", "fside_BxSxS_0", "cond_512", "L0_cond_w", "L0_cond_u", "L0_attn_W_in", "L0_attn_b_in",
        "L0_attn_W_decay", "L0_attn_b_decay", "L0_attn_W_gate", "L0_attn_b_gate", "L0_attn_W_out",
        "L0_attn_b_out", "L0_attn_decay_bias", "L0_cond2_w", "L0_cond2_u", "L0_ffn_Wg", "L0_ffn_w1", "L0_ffn_w2"]


def kernel(**inputs):
    import numpy as _np
    import concourse.bacc as _bacc
    from concourse import mybir as _mybir
    from concourse.bass_utils import run_bass_kernel_spmd as _run

    nc = _bacc.Bacc("TRN2", target_bir_lowering=False, num_devices=1)
    arrays, args = {}, []
    for name in _INS:
        a = _np.ascontiguousarray(inputs[name])
        arrays[f"in_{name}_dram"] = a
        args.append(nc.dram_tensor(f"in_{name}_dram", a.shape, _mybir.dt.from_np(a.dtype), kind="ExternalInput").ap())
    args.append(nc.dram_tensor("out_0_dram", (B, T, C), _mybir.dt.float32, kind="ExternalOutput").ap())
    build_program(nc, *args)
    r = _run(nc, [arrays], core_ids=[0])
    return r.results[0]["out_0_dram"]
```

```python
from contextlib import ExitStack
import math

import concourse.bass as bass
from concourse import mybir

F32 = mybir.dt.float32
F32R = mybir.dt.float32r
BF16 = mybir.dt.bfloat16
I32 = mybir.dt.int32
U32 = mybir.dt.uint32
ALU = mybir.AluOpType
ACT = mybir.ActivationFunctionType
AX = mybir.AxisListType

P = 128
B, T, C = 4, 512, 512
CT = C // P
TT = T // P
NE, DFF, TOPK = 8, 2048, 2
CAP = math.ceil(1.25 * B * T * TOPK / NE)
ST = CAP // P
ROW = C + NE + 1
NO_TOKEN = 1 << 20
CAPV, DEN_MIN = 30.0, 1e-8
FT = DFF // P
FC = 4
NC = FT // FC
PIECES = 2 * FC
W1C, W2C, U1C, U2C, BIN, BGATE, BOUT, BDEC, DBIAS = range(9)


GATE_TILES = [(0, e) for e in range(CT)] + [(m, e) for e in range(CT) for m in (1, 2)]
IN_PSUM = 2
Z_COPIES = len(GATE_TILES) - IN_PSUM


def first_batch(b):
    return isinstance(b, int) and b == 0


def at_least(b, n):
    return not isinstance(b, int) or b >= n


class Steps:

    def __init__(self, eng, sem, base):
        self.eng, self.sem, self.base, self.n = eng, sem, base, 0

    def mark(self, ins):
        ins.then_inc(self.sem, 1)
        self.n += 1

    def wait(self):
        self.eng.wait_ge(self.sem, self.base + self.n)

    def do(self, ins):
        self.mark(ins)
        self.wait()


def build_program(nc, x, fside, cond, w1c, u1c, W_in, b_in, W_decay, b_decay, W_gate, b_gate,
                  W_out, b_out, decay_bias, w2c, u2c, Wg, w1, w2, out):
    slots = nc.dram_tensor("slots", ((NE + 1) * CAP, ROW), F32, kind="Internal").ap()
    out_rows = out.rearrange("b t c -> (b t) c")
    with ExitStack() as ctx:
        def sb(name, shape, dt=F32):
            return ctx.enter_context(nc.sbuf_tensor(name, shape, dt))

        ident = sb("ident", [P, P])
        counts = sb("counts", [P, NE], I32)
        rows = sb("rows", [P, ST, ROW])
        with ExitStack() as early:
            cond_buffers = [early.enter_context(nc.sbuf_tensor(name, [P, 4, T], F32))
                            for name in ("scaled", "k_and_exp_k", "euk", "eukv", "sums_even", "sums_odd")]
        with ExitStack() as early:
            gate_parts = [early.enter_context(nc.sbuf_tensor(name, [P, CT, C], F32R)) for name in (
                "r1_high", "r1_low", "w_decay_high", "w_decay_low", "w_gate_high", "w_gate_low")]
        place0 = [sb(name, [P, FC, C], F32 if name[0] == "r" else F32R)
                  for name in ("raw1_0", "raw2_0", "w1h_0", "w1l_0", "w2h_0", "w2l_0")]
        load_sems = [ctx.enter_context(nc.semaphore(name)) for name in (
            "weights_in_even", "weights_in_odd", "rows_in", "weights_high", "weights_low",
            *(f"first_rows_in_{i}" for i in range(ST - 1)))]
        with ExitStack() as phase:
            conditioning_and_routing(nc, phase, ident, counts, rows, cond_buffers, gate_parts, place0, load_sems,
                                     slots, out_rows, x, fside, cond, w1c, u1c,
                                     W_in, b_in, W_decay, b_decay, W_gate, b_gate, W_out, b_out,
                                     decay_bias, w2c, u2c, Wg, w1, w2)
        with ExitStack() as phase:
            experts(nc, phase, ident, counts, rows, place0, load_sems, slots, out_rows, w1, w2)


def load_chunk(sp, sems, raw1, raw2, w1, w2, e, c):
    hidden = slice(c * FC * P, (c + 1) * FC * P)
    sp.dma_start(raw1, w1[bass.ds(e, 1), :, hidden].rearrange("o (t p) f -> p (o t) f", p=P)).then_inc(sems[c % 2], 16)
    sp.dma_start(raw2, w2[bass.ds(e, 1), hidden, :].rearrange("o (t p) n -> p (o t) n", p=P)).then_inc(sems[c % 2], 16)


def load_slot_rows(sp, sem, rows, slots, e):
    sp.dma_start(rows[:], slots[bass.ds(e * CAP, CAP)].rearrange("(i p) c -> p i c", p=P)).then_inc(sem, 16)


def pieces(place):
    raw1, raw2, w1h, w1l, w2h, w2l = place
    return ([(raw1[:, n], w1h[:, n], w1l[:, n]) for n in range(CT)] +
            [(raw2[:, n], w2h[:, n], w2l[:, n]) for n in range(FC)])


def weight_high(nc, piece, s_wh):
    raw, high, _ = piece
    nc.scalar.activation(high, raw, ACT.Copy).then_inc(s_wh, 1)


def weight_low(nc, piece, s_wl):
    raw, high, low = piece
    nc.vector.tensor_tensor(low, raw, high.bitcast(F32), ALU.subtract).then_inc(s_wl, 1)


def conditioning_and_routing(nc, ctx, ident, counts, rows, cond_buffers, gate_parts, place0, load_sems,
                             slots, out_rows, x, fside, cond, w1c, u1c,
                             W_in, b_in, W_decay, b_decay, W_gate, b_gate, W_out, b_out,
                             decay_bias, w2c, u2c, Wg, w1, w2):
    def sb(name, shape, dt=F32):
        return ctx.enter_context(nc.sbuf_tensor(name, shape, dt))

    def ps(name, shape, dt=F32):
        return ctx.enter_context(nc.psum_tensor(name, shape, dt))

    def sem(name):
        return ctx.enter_context(nc.semaphore(name))

    lower = sb("lower", [P, P], BF16)
    ones = sb("ones", [P, P], BF16)
    expert_no = sb("expert_no", [P, TT, NE])
    slot_base = sb("slot_base", [P, TT, NE])
    token_no = sb("token_no", [P, B * TT], U32)
    vec = sb("vec", [P, 9, CT])
    wm = sb("wm", [P, 4, CT, C])
    wg = sb("wg", [P, CT, NE])
    tf = sb("tf", [P, B])
    half_tf = sb("half_tf", [P, B])
    neg_scale = sb("neg_scale", [P, B])
    ew = sb("ew", [P, 2, CT])
    decay = sb("decay", [P, B * 2 * CT])
    one_m = sb("one_m", [P, B * 2 * CT])
    one_md2 = sb("one_md2", [P, B * 2 * CT])
    bdec = sb("bdec", [P, CT])
    x_rows = rows[:, 0:TT, 0:C]
    f_rows = sb("f_rows", [P, TT, C])
    xT = sb("xT", [P, 2, CT, T])
    kT = cond_buffers[1][:, 0:2]
    ek = cond_buffers[1][:, 2:4]
    ekv = sb("ekv", [P, 2, T])
    euk, eukv = (cond_buffers[n][:].rearrange("p (r c) t -> p r c t", r=2) for n in (2, 3))
    sums = [cond_buffers[n][:].rearrange("p (c n) t -> p c n t", c=2) for n in (4, 5)]
    scaled = cond_buffers[0][:].rearrange("p (c n) t -> p c n t", c=2)
    recip0 = sb("recip0", [P, 2, T])
    r1T = sb("r1T", [P, 2, CT, T])
    ratio2 = sb("ratio2", [P, 2, CT, T])
    sig = sb("sig", [P, CT, T])
    z_in = sb("z_in", [P, CT, T])
    z_dec = sb("z_dec", [P, CT, T])
    z_gate = sb("z_gate", [P, CT, T])
    x2_rows = sb("x2_rows", [P, TT, C])
    r2_rows = sb("r2_rows", [P, TT, ROW])
    logit = sb("logit", [P, TT, NE])
    top = sb("top", [P, TT, NE])
    top_i = sb("top_i", [P, TT, NE], U32)
    top_f = sb("top_f", [P, TT, NE])
    oh = sb("oh", [P, 2, TT, NE])
    sel = sb("sel", [P, TT, NE], BF16)
    carry = sb("carry", [P, NE], BF16)
    sel_sum = sb("sel_sum", [P, NE])
    pe_ = sb("prob", [P, TT, NE])
    psum_ = sb("prob_sum", [P, TT])
    slot_f = sb("slot_f", [P, TT, NE])
    slot_t = sb("slot_t", [P, TT, NE])
    dest_f = sb("dest_f", [P, 2, TT])
    dest = sb("dest", [P, 2, TT], U32)

    ps_f = ps("ps_f", [P, T])
    ps_x = ps("ps_x", [P, T])
    ps_mm = ps("ps_mm", [P, 3, T])
    bank = lambda e: ps_x[:] if e == 1 else ps_mm[:, (0, None, 1, 2)[e], :]
    ps_to = ps("ps_to", [P, C])
    row_bank = lambda i, banks: (ps_to, ps_x)[i % banks]
    ps_small = ps("ps_small", [P, 512])
    ps_logit = ps_small[:, 0:32].rearrange("p (i e) -> p i e", i=TT)
    ps_pos = ps_small[:, 32:64].rearrange("p (i e) -> p i e", i=TT)
    ps_count = ps_small[:, 64:72]
    ps_decay = ps("ps_decay", [P, 512])[:, 0:B * 2 * CT]

    s_vec, s_w, s_f_in, s_x_in = sem("vec_in"), sem("w_in"), sem("f_in"), sem("x_in")
    s_init, s_x2_out, s_x2_free, s_disp = sem("slots_init"), sem("x2_out"), sem("x2_rows_free"), sem("dispatched")
    s_pool_setup, s_template, s_consts = sem("pool_setup"), sem("template"), sem("consts_ready")
    s_setup_v, s_setup_a = sem("setup_dve"), sem("setup_act")
    s_f_tp, s_x_tp, s_k, s_xT = sem("f_transposed"), sem("x_transposed"), sem("k_ready"), sem("xT_ready")
    s_caps, s_ek, s_euk, s_ekv, s_eukv = sem("caps_ready"), sem("ek_ready"), sem("euk_ready"), sem("ekv_ready"), sem("eukv_ready")
    s_bwd, s_scaled, s_den, s_ln, s_rec, s_newton, s_ratio = (
        sem("bwd_done"), sem("scaled_ready"), sem("den_ready"), sem("ln_ready"), sem("recip_ready"),
        sem("newton_ready"), sem("ratio_ready"))
    s_own = sem("numerator_own_term")
    s_gh, s_gl = sem("gate_operands_high"), sem("gate_operands_low")
    s_fold, s_vt = sem("fold_steps"), sem("vectors_transposed")
    s_sig1, s_r1, s_mm, s_z, s_gates = sem("sig1_ready"), sem("r1_ready"), sem("mm_done"), sem("z_ready"), sem("gates_ready")
    s_rec_steps, s_y, s_wo, s_x2, s_sig2, s_r2 = (
        sem("recurrence_steps"), sem("y_ready"), sem("wout_done"), sem("x2_ready"), sem("sig2_ready"), sem("r2_ready"))
    s_to, s_ev_x2, s_ev_r2, s_logit = sem("rows_transposed"), sem("x2_rows_ready"), sem("r2_rows_ready"), sem("logits_done")
    s_route, s_shift, s_pexp, s_sel, s_pos, s_dest, s_count = (
        sem("route_steps"), sem("shift_ready"), sem("prob_exp"), sem("sel_ready"), sem("pos_done"), sem("dest_ready"), sem("count_done"))

    N_V = 9
    N_VEC = N_V + 1
    ROUTE_STEPS = 17 + 2 * TT
    vec_cond = z_gate[:, 0, :]
    vec_rows = z_gate[0:N_V * CT, 1, 0:P]
    block = ctx.enter_context(nc.Block())

    def gate_piece(n):
        which, dt = divmod(n, CT)
        high, low = gate_parts[2 * which:2 * which + 2]
        raw = r1T[:, (B - 1) % 2, dt, :] if which == 0 else wm[:, which, dt, :]
        return raw, high[:, dt], low[:, dt]

    def col(b, c, ct):
        return bass.ds(b * (2 * CT) + (c * CT + ct), 1)

    @block.sync
    def _(sp):
        def load_f(b):
            sp.dma_start(f_rows[:], fside[bass.ds(b, 1)].rearrange("o (i p) c -> p (o i) c", p=P)).then_inc(s_f_in, 16)

        def load_x(b):
            sp.dma_start(x_rows, x[bass.ds(b, 1)].rearrange("o (i p) c -> p (o i) c", p=P)).then_inc(s_x_in, 16)

        def store(b):
            sp.wait_ge(s_ev_x2, TT * (b + 1))
            sp.dma_start(out_rows[bass.ds(b * T, T)].rearrange("(i p) c -> p i c", p=P), x2_rows[:]).then_inc(s_x2_out, 16)
            sp.wait_ge(s_x2_out, 16 * (b + 1))
            sp.sem_inc(s_x2_free, 1)

        def load_w(n):
            sp.dma_start(wm[:, n], (W_in, W_decay, W_gate, W_out)[n].rearrange("(t p) n -> p t n", p=P)).then_inc(s_w, 16)

        def clear_slots(first, last):
            for e in range(first, last):
                sp.dma_start(slots[e * CAP:(e + 1) * CAP, :].rearrange("(p i) c -> p i c", i=ST),
                             r2_rows[:, 0:1, :].to_broadcast([P, ST, ROW])).then_inc(s_init, 16)

        sp.sem_inc(s_x2_free, 1)
        sp.dma_start(vec_cond[:], cond.rearrange("b d -> (b d)").partition_broadcast(P)).then_inc(s_vec, 16)
        for n, vector in ((W1C, w1c), (W2C, w2c), (U1C, u1c), (U2C, u2c), (BIN, b_in), (BGATE, b_gate),
                          (BOUT, b_out), (BDEC, b_decay), (DBIAS, decay_bias)):
            sp.dma_start(vec_rows[n * CT:(n + 1) * CT, :], vector.rearrange("(t p) -> t p", p=P)).then_inc(s_vec, 16)
        load_f(0)
        load_x(0)
        load_w(0)
        load_w(1)
        sp.wait_ge(s_f_tp, CT)
        load_f(1)
        load_w(2)
        load_w(3)
        sp.dma_start(wg[:], Wg.rearrange("(t p) e -> p t e", p=P)).then_inc(s_w, 16)
        sp.wait_ge(s_x_tp, CT)
        load_x(1)
        sp.wait_ge(s_template, 2)
        clear_slots(1, NE // 2)
        for b in range(2, B):
            sp.wait_ge(s_f_tp, b * CT)
            load_f(b)
            sp.wait_ge(s_x_tp, b * CT)
            load_x(b)
            if b == 2:
                clear_slots(NE // 2, NE + 1)
        store(0)
        sp.wait_ge(s_f_tp, B * CT)
        load_f(B - 1)
        with sp.Fori(1, B - 1) as b:
            store(b)
        sp.wait_ge(s_mm, len(GATE_TILES) * B)
        load_chunk(sp, load_sems, place0[0][:], place0[1][:], w1, w2, 0, 0)
        store(B - 1)
        sp.wait_ge(s_x_tp, B * CT)
        sp.wait_ge(s_disp, 16 * (1 + TT * TOPK * B))
        for i in range(ST):
            sp.dma_start(rows[:, i], slots[i * P:(i + 1) * P]).then_inc(load_sems[5 + i] if i < ST - 1 else load_sems[2], 16)
        sp.wait_ge(s_f_in, 16 * (B + 1))
        sp.wait_ge(s_x2_out, 16 * B)
        sp.wait_ge(s_init, 16 * NE)

    @block.gpsimd
    def _(pool):
        g = nc.gpsimd
        setup = Steps(pool, s_pool_setup, 0)
        setup.mark(g.memset(ident[:], 0.0))
        setup.mark(g.memset(lower[:], 1.0))
        setup.do(g.memset(ones[:], 1.0))
        setup.mark(g.affine_select(out=ident[:], in_=ident[:], compare_op=ALU.not_equal, fill=1.0, base=0,
                                   pattern=[[-1, P]], channel_multiplier=1))
        setup.mark(g.affine_select(out=lower[:], in_=lower[:], compare_op=ALU.is_gt, fill=0.0, base=0,
                                   pattern=[[1, P]], channel_multiplier=-1))
        setup.mark(g.iota(expert_no[:], [[0, TT], [1, NE]], base=0, channel_multiplier=0,
                          allow_small_or_imprecise_dtypes=True))
        setup.mark(g.iota(slot_base[:], [[0, TT], [CAP, NE]], base=0, channel_multiplier=0,
                          allow_small_or_imprecise_dtypes=True))
        setup.mark(g.iota(token_no[:], [[P, B * TT]], base=0, channel_multiplier=1))
        g.memset(carry[:], 0.0).then_inc(s_consts, 1)

        def products(u, ct):
            r = ct % 2
            pool.wait_ge(s_ek, u + 1)
            if not isinstance(u, int) or u >= 2:
                pool.wait_ge(s_den, u - 1)
            g.tensor_tensor(ekv[:, r], ek[:, r], kT[:, r], ALU.mult).then_inc(s_ekv, 1)
            pool.wait_ge(s_euk, u + 1)
            g.tensor_tensor(eukv[:, r, 0], euk[:, r, 0], kT[:, r], ALU.mult)
            g.tensor_tensor(eukv[:, r, 1], euk[:, r, 1], kT[:, r], ALU.mult).then_inc(s_eukv, 1)

        def newton(u, ct):
            r = ct % 2
            pool.wait_ge(s_den, u + 1)
            pool.wait_ge(s_eukv, u + 1)
            for c in range(2):
                g.tensor_tensor(sums[r][:, c, 0], sums[r][:, c, 0], eukv[:, r, c], ALU.add).then_inc(s_own, 1)
                pool.wait_ge(s_rec, 2 * u + c + 1)
                pool.wait_ge(s_own, 2 * u + c + 1)
                g.tensor_tensor(sums[r][:, c, 1], sums[r][:, c, 1], recip0[:, c], ALU.mult)
                g.tensor_tensor(sums[r][:, c, 0], sums[r][:, c, 0], recip0[:, c], ALU.mult).then_inc(s_newton, 1)

        def conditioning(b):
            for s in range(CT + 1):
                if s >= 1:
                    newton(b * CT + (s - 1), s - 1)
                if s < CT:
                    products(b * CT + (s + 1), (s + 1) % CT)

        def dispatch(b):
            pool.wait_ge(s_dest, b + 1)
            pool.wait_ge(s_init, 16 * NE)
            pool.wait_ge(s_disp, 16 * (1 + TT * TOPK * b))
            for i in range(TT):
                pool.wait_ge(s_ev_r2, TT * b + i + 1)
                pool.nop(nofuse=True)
                for k in range(TOPK):
                    pool.indirect_dma_start(
                        out=slots, out_offset=bass.IndirectOffsetOnAxis(ap=dest[:, k, i:i + 1], axis=0),
                        in_=r2_rows[:, i, :], in_offset=None, bounds_check=NE * CAP - 1, oob_is_err=False,
                    ).then_inc(s_disp, 16)

        products(0, 0)
        pool.wait_ge(s_template, 2)
        pool.dma_start(slots[0:CAP, :].rearrange("(p i) c -> p i c", i=ST),
                       r2_rows[:, 0:1, :].to_broadcast([P, ST, ROW])).then_inc(s_disp, 16)
        conditioning(0)
        conditioning(1)
        with pool.Fori(2, B) as b:
            conditioning(b)
            dispatch(b - 2)
        dispatch(B - 2)
        dispatch(B - 1)
        pool.wait_ge(s_disp, 16 * (1 + TT * TOPK * B))

    @block.tensor
    def _(pe):
        def transpose_f(b, ct):
            u = b * CT + ct
            if ct == 0:
                pe.wait_ge(s_f_in, 16 * (b + 1))
            if not (isinstance(u, int) and u == 0):
                pe.wait_ge(s_k, u)
            for i in range(TT):
                last = nc.tensor.transpose(ps_f[:, i * P:(i + 1) * P], f_rows[:, i, ct * P:(ct + 1) * P], ident[:])
            last.then_inc(s_f_tp, 1)

        def transpose_x(b, ct):
            if ct == 0:
                pe.wait_ge(s_x_in, 16 * (b + 1))
                if at_least(b, 2):
                    pe.wait_ge(s_ev_x2, TT * (b - 1))
            if not (first_batch(b) and ct == 0):
                pe.wait_ge(s_xT, b * CT + ct)
            for i in range(TT):
                last = nc.tensor.transpose(ps_x[:, i * P:(i + 1) * P], x_rows[:, i, ct * P:(ct + 1) * P], ident[:])
            last.then_inc(s_x_tp, 1)

        def gate(b, k):
            m, e = GATE_TILES[k]
            if k == 0:
                pe.wait_ge(s_r1, b + 1)
            if k < 3 and at_least(b, 1):
                pe.wait_ge(s_x2, CT * (b - 1) + (1, 3, 4)[k])
            if k >= 3:
                pe.wait_ge(s_z, Z_COPIES * b + k - 2)
            if isinstance(b, int) and b == B - 1 and k >= CT:
                pe.wait_ge(s_gl, 3 * CT)
                high, low = gate_parts[2 * m], gate_parts[2 * m + 1]
                column = slice(e * P, (e + 1) * P)
                for dt in range(CT):
                    nc.tensor.matmul(ps_mm[:, k % 3, :], high[:, dt, column], gate_parts[0][:, dt], start=(dt == 0), stop=False)
                    nc.tensor.matmul(ps_mm[:, k % 3, :], high[:, dt, column], gate_parts[1][:, dt], start=False, stop=False)
                    last = nc.tensor.matmul(ps_mm[:, k % 3, :], low[:, dt, column], gate_parts[0][:, dt], start=False, stop=(dt == CT - 1))
                last.then_inc(s_mm, 1)
                return
            for dt in range(CT):
                last = nc.tensor.matmul(ps_mm[:, k % 3, :], wm[:, m, dt, e * P:(e + 1) * P],
                                        r1T[:, bass.ds(b % 2, 1), dt, :].rearrange("p o t -> p (o t)"),
                                        start=(dt == 0), stop=(dt == CT - 1))
            last.then_inc(s_mm, 1)

        def project(b, x_done):
            for dt in range(CT):
                pe.wait_ge(s_y, CT * b + dt + 1)
                for e in range(CT):
                    if dt == 0 and e == 1:
                        pe.wait_ge(s_xT, CT * x_done)
                    if dt == 0 and e == 2:
                        pe.wait_ge(s_gates, CT * (b + 1))
                    last = nc.tensor.matmul(bank(e), wm[:, 3, dt, e * P:(e + 1) * P], z_gate[:, dt, :],
                                            start=(dt == 0), stop=(dt == CT - 1))
                    if dt == CT - 1:
                        last.then_inc(s_wo, 1)

        def x2_row(b, i):
            if i < 2:
                pe.wait_ge(s_x2, CT * (b + 1))
            else:
                pe.wait_ge(s_ev_x2, TT * b + i - 1)
            for ct in range(CT):
                last = nc.tensor.transpose(row_bank(i, 2)[:, ct * P:(ct + 1) * P], z_dec[:, ct, i * P:(i + 1) * P], ident[:])
            last.then_inc(s_to, 1)

        def r2_row(b, i, banks):
            if i < banks:
                pe.wait_ge(s_r2, b + 1)
                pe.wait_ge(s_ev_x2, TT * (b + 1))
            else:
                pe.wait_ge(s_ev_r2, TT * b + i + 1 - banks)
            for ct in range(CT):
                last = nc.tensor.transpose(row_bank(i, banks)[:, ct * P:(ct + 1) * P], sig[:, ct, i * P:(i + 1) * P], ident[:])
            last.then_inc(s_to, 1)

        def logits(b):
            pe.wait_ge(s_r2, b + 1)
            for i in range(TT):
                for ct in range(CT):
                    last = nc.tensor.matmul(ps_logit[:, i, :], sig[:, ct, i * P:(i + 1) * P], wg[:, ct, :],
                                            start=(ct == 0), stop=(ct == CT - 1))
            last.then_inc(s_logit, 1)

        def places(b):
            pe.wait_ge(s_sel, b + 1)
            for i in range(TT):
                nc.tensor.matmul(ps_pos[:, i, :], lower[:], sel[:, i, :], start=True, stop=False)
                for j in range(i):
                    nc.tensor.matmul(ps_pos[:, i, :], ones[:], sel[:, j, :], start=False, stop=False)
                last = nc.tensor.matmul(ps_pos[:, i, :], ones[:], carry[:], start=False, stop=True)
            last.then_inc(s_pos, 1)

        def step(b, cond, gates, tail):
            banks = 1 if gates else 2
            if cond:
                transpose_f(b, 1)
            if tail:
                project(b - 2, b if cond else B)
            if cond:
                transpose_f(b, 2)
            for k in range(len(GATE_TILES)):
                if gates:
                    gate(b - 1, k)
                if tail and k < TT:
                    x2_row(b - 2, k)
                if tail and k == 5:
                    logits(b - 2)
                if tail and 5 <= k <= 8:
                    r2_row(b - 2, k - 5, banks)
                if cond and k == 2:
                    transpose_f(b, 3)
                if cond and k == 5:
                    transpose_f(b + 1, 0)
                if cond and 6 <= k <= 9:
                    transpose_x(b, k - 6)
                if tail and k == (9 if gates else 6):
                    places(b - 2)

        pe.wait_ge(s_pool_setup, 8)
        pe.wait_ge(s_vec, 16 * N_VEC)
        nc.tensor.transpose(ps_small[:, 0:N_V * CT], vec_rows, ident[0:N_V * CT, 0:N_V * CT]).then_inc(s_vt, 1)

        transpose_f(0, 0)
        step(0, True, False, False)
        pe.wait_ge(s_consts, 2)
        pe.wait_ge(s_w, 16 * 5)
        step(1, True, True, False)
        with pe.Fori(2, B) as b:
            step(b, True, True, True)
        step(B, False, True, True)
        step(B + 1, False, False, True)
        pe.wait_ge(s_dest, B)
        nc.tensor.matmul(ps_count, ones[:], carry[:], start=True, stop=True).then_inc(s_count, 1)

    @block.scalar
    def _(act):
        a = nc.scalar

        def copy_f(b, ct):
            u = b * CT + ct
            act.wait_ge(s_f_tp, u + 1)
            if at_least(u, 2):
                act.wait_ge(s_eukv, u - 1)
            a.activation(kT[:, ct % 2], ps_f[:], ACT.Copy).then_inc(s_k, 1)

        def copy_x(b, ct):
            act.wait_ge(s_x_tp, b * CT + ct + 1)
            if ct == 0 and at_least(b, 2):
                act.wait_ge(s_x2, CT * (b - 1))
            act.nop(nofuse=True)
            a.activation(xT[:, bass.ds(b % 2, 1), ct, :], ps_x[:].rearrange("p (o t) -> p o t", o=1),
                         ACT.Copy).then_inc(s_xT, 1)

        def exps(b, ct):
            u, r = b * CT + ct, ct % 2
            act.wait_ge(s_caps, u + 1)
            a.activation(ek[:, r], ek[:, r], ACT.Exp).then_inc(s_ek, 1)
            a.activation(euk[:, r], euk[:, r], ACT.Exp).then_inc(s_euk, 1)

        def scale(b, ct):
            u, r = b * CT + ct, ct % 2
            if at_least(u, 1):
                act.wait_ge(s_den, u)
            for c in range(2):
                act.wait_ge(s_bwd, 2 * u + c + 1)
                a.activation(scaled[:, c, :, 1:T], sums[r][:, c, :, 1:T], ACT.Copy,
                             scale=one_md2[:, col(b, c, ct)]).then_inc(s_scaled, 1)

        def first_reciprocal(b, ct):
            u, r = b * CT + ct, ct % 2
            act.wait_ge(s_den, u + 1)
            if not isinstance(b, int) or u >= 1:
                act.wait_ge(s_newton, 2 * u)
            for c in range(2):
                a.activation(recip0[:, c], sums[r][:, c, 1], ACT.Ln).then_inc(s_ln, 1)
            for c in range(2):
                act.wait_ge(s_ln, 2 * u + c + 1)
                a.activation(recip0[:, c], recip0[:, c], ACT.Exp, scale=-1.0).then_inc(s_rec, 1)

        def gate_source(k):
            m, e = GATE_TILES[k]
            return (z_in, z_dec, z_gate)[m], (vec[:, BIN, e:e + 1], bdec[:, e:e + 1], vec[:, BGATE, e:e + 1])[m], e

        def gate_sum(b, k):
            if k == 0 and at_least(b, 1):
                act.wait_ge(s_wo, CT * b)
            if k == CT and at_least(b, 1):
                act.wait_ge(s_to, 2 * TT * (b - 1) + TT)
                act.wait_ge(s_sig2, b)
            z, bias, e = gate_source(k)
            act.wait_ge(s_mm, 12 * b + k + 1)
            a.activation(z[:, e], ps_mm[:, k % 3, :], ACT.Identity, bias=bias).then_inc(s_z, 1)

        def inputs(b):
            act.wait_ge(s_z, Z_COPIES * b + CT)
            a.activation(z_in[:], z_in[:], ACT.Silu)

        def gate_functions(b):
            act.wait_ge(s_z, Z_COPIES * (b + 1))
            for k in range(CT, len(GATE_TILES)):
                z, bias, e = gate_source(k)
                if k < Z_COPIES:
                    last = a.activation(z[:, e], z[:, e], ACT.Sigmoid)
                else:
                    act.wait_ge(s_mm, 12 * b + k + 1)
                    last = a.activation(z[:, e], ps_mm[:, k % 3, :], ACT.Sigmoid, bias=bias)
                if GATE_TILES[k][0] == 2:
                    last.then_inc(s_gates, 1)

        def sigmoid_x(b):
            act.wait_ge(s_xT, CT * (b + 1))
            if at_least(b, 1):
                act.wait_ge(s_r1, b)
            if at_least(b, 2):
                act.wait_ge(s_to, 2 * TT * (b - 1))
            act.nop(nofuse=True)
            a.activation(sig[:], xT[:, bass.ds(b % 2, 1)].rearrange("p o c t -> p (o c) t"), ACT.Sigmoid).then_inc(s_sig1, 1)

        def sigmoid_x2(b, r1_done):
            act.wait_ge(s_x2, CT * (b + 1))
            act.wait_ge(s_r1, r1_done)
            a.activation(sig[:], z_dec[:], ACT.Sigmoid).then_inc(s_sig2, 1)

        def x2_row(b, i):
            if i == 0:
                act.wait_ge(s_x2_free, b + 1)
            act.wait_ge(s_to, 2 * TT * b + i + 1)
            a.activation(x2_rows[:, i], row_bank(i, 2)[:], ACT.Copy).then_inc(s_ev_x2, 1)

        def r2_row(b, i, banks):
            if i == 0:
                act.wait_ge(s_init, 16 * NE)
                act.wait_ge(s_disp, 16 * (1 + TT * TOPK * b))
            act.wait_ge(s_to, 2 * TT * b + TT + i + 1)
            a.activation(r2_rows[:, i, 0:C], row_bank(i, banks)[:], ACT.Copy).then_inc(s_ev_r2, 1)

        def probabilities(b):
            act.wait_ge(s_shift, b + 1)
            a.activation(pe_[:], pe_[:], ACT.Exp).then_inc(s_pexp, 1)

        def step(b, cond, gates, tail):
            banks = 1 if gates else 2
            def sums_of(ks):
                if gates:
                    for k in ks:
                        gate_sum(b - 1, k)

            def unit(s):
                if cond:
                    copy_f(b if s + 1 < CT else b + 1, (s + 1) % CT)
                    if s >= 1:
                        first_reciprocal(b, s - 1)
                    scale(b, s)
                    exps(b if s + 1 < CT else b + 1, (s + 1) % CT)

            if cond:
                act.preload_act_table_set("natural_log_exp_and_others")
            if gates and not cond:
                act.wait_ge(s_ratio, 2 * B * CT)
                act.wait_ge(s_eukv, B * CT + 1)
                act.wait_ge(s_w, 16 * 5)
                act.wait_ge(s_r1, B)
                for n in range(3 * CT):
                    raw, high, _ = gate_piece(n)
                    a.activation(high, raw, ACT.Copy).then_inc(s_gh, 1)
            unit(0)
            sums_of([0])
            if tail and gates:
                x2_row(b - 2, 0)
            unit(1)
            sums_of([1])
            if tail and gates:
                x2_row(b - 2, 1)
            if tail:
                sigmoid_x2(b - 2, b if cond else B)
                act.preload_act_table_set("natural_log_exp_and_others")
            if tail and not gates:
                x2_row(b - 2, 0)
                x2_row(b - 2, 1)
            sums_of([2])
            if tail:
                x2_row(b - 2, 2)
            unit(2)
            for k in (3, 4, 5, 6):
                sums_of([k])
                if tail and k == 3:
                    x2_row(b - 2, k)
                if tail and k >= 5:
                    r2_row(b - 2, k - 5, banks)
            if cond:
                copy_x(b, 0)
            unit(3)
            for k in (7, 8):
                sums_of([k])
                if tail:
                    r2_row(b - 2, k - 5, banks)
                if cond:
                    copy_x(b, k - 6)
            if tail:
                probabilities(b - 2)
            if cond:
                first_reciprocal(b, CT - 1)
            if gates:
                inputs(b - 1)
            sums_of([9])
            if cond:
                copy_x(b, CT - 1)
            if gates:
                gate_functions(b - 1)
            if cond:
                sigmoid_x(b)

        act.wait_ge(s_setup_v, 1)
        setup = Steps(act, s_setup_a, 0)
        setup.do(a.activation(ew[:], vec[:, W1C:W2C + 1, :], ACT.Exp))
        setup.do(a.activation(ew[:], ew[:], ACT.Exp, scale=-1.0))
        act.wait_ge(s_setup_v, 2)
        setup.do(a.activation(tf[:], tf[:], ACT.Sigmoid))
        act.preload_act_table_set("natural_log_exp_and_others")
        copy_f(0, 0)
        exps(0, 0)
        act.wait_ge(s_consts, 2)
        step(0, True, False, False)
        step(1, True, True, False)
        with act.Fori(2, B) as b:
            step(b, True, True, True)
        step(B, False, True, True)
        step(B + 1, False, False, True)
        act.wait_ge(load_sems[0], 32)
        for piece in pieces(place0):
            weight_high(nc, piece, load_sems[3])

    @block.vector
    def _(dve):
        v = nc.vector
        d0 = lambda b, c, ct, n: ps_decay[:, col(b, c, ct)].to_broadcast([P, n])

        def caps(b, ct):
            u, r = b * CT + ct, ct % 2
            dve.wait_ge(s_k, u + 1)
            if at_least(u, 2):
                dve.wait_ge(s_den, u - 1)
            v.tensor_scalar(ek[:, r], kT[:, r], CAPV, None, ALU.min)
            for c in range(2):
                last = v.tensor_scalar(euk[:, r, c], kT[:, r], vec[:, U1C + c, ct:ct + 1], CAPV, ALU.add, ALU.min)
            last.then_inc(s_caps, 1)

        setup = Steps(dve, s_setup_v, 0)
        dve.wait_ge(s_vt, 1)
        setup.do(v.tensor_copy(vec[:].rearrange("p n t -> p (n t)"), ps_small[:, 0:N_V * CT]))
        dve.wait_ge(s_vec, 16 * N_VEC)
        setup.mark(v.tensor_reduce(tf[:], vec_cond.rearrange("p (b d) -> p b d", b=B), AX.X, ALU.add))
        setup.mark(v.tensor_tensor(bdec[:], vec[:, BDEC], vec[:, DBIAS], ALU.add))
        dve.wait_ge(s_setup_a, 3)
        setup.mark(v.tensor_scalar(half_tf[:], tf[:], 0.5, 0.5, ALU.mult, ALU.add))
        setup.mark(v.tensor_scalar(neg_scale[:], tf[:], 0.2, 0.8, ALU.mult, ALU.add))
        setup.wait()
        setup.mark(v.tensor_scalar(neg_scale[:], neg_scale[:], -1.0, None, ALU.mult))
        for b in range(B):
            setup.mark(v.tensor_scalar(decay[:, b * 2 * CT:(b + 1) * 2 * CT], ew[:].rearrange("p c t -> p (c t)"),
                                       half_tf[:, b:b + 1], None, ALU.mult))
        caps(0, 0)
        setup.wait()
        setup.mark(v.tensor_copy(ps_decay, decay[:]))
        setup.mark(v.tensor_scalar(one_m[:], decay[:], -1.0, 1.0, ALU.mult, ALU.add))
        setup.wait()
        v.scalar_tensor_tensor(out=one_md2[:], in0=decay[:], scalar=1.0, in1=one_m[:], op0=ALU.add,
                               op1=ALU.mult).then_inc(s_consts, 1)
        v.memset(r2_rows[:, 0], 0.0).then_inc(s_template, 1)
        dve.wait_ge(s_template, 1)
        v.memset(r2_rows[:, 0, C + NE:ROW].bitcast(U32), NO_TOKEN).then_inc(s_template, 1)

        def backward(b, ct):
            u, r = b * CT + ct, ct % 2
            dve.wait_ge(s_ekv, u + 1)
            if at_least(u, 2):
                dve.wait_ge(s_ratio, 2 * (u - 1))
            for c in range(2):
                v.tensor_tensor_scan(sums[r][:, c, 1, ::-1], d0(b, c, ct, T), ek[:, r, ::-1], 0.0, ALU.mult, ALU.add)
                v.tensor_tensor_scan(sums[r][:, c, 0, ::-1], d0(b, c, ct, T), ekv[:, r, ::-1], 0.0, ALU.mult, ALU.add).then_inc(s_bwd, 1)

        def fold(b, ct):
            u, r = b * CT + ct, ct % 2
            steps = Steps(dve, s_fold, 4 * u)
            for c in range(2):
                dve.wait_ge(s_scaled, 2 * u + c + 1)
                for n in range(2):
                    s = sums[r][:, c, n]
                    ins = v.tensor_tensor_scan(s[:, 1:T], d0(b, c, ct, T - 1), scaled[:, c, n, 1:T], s[:, 0:1], ALU.mult, ALU.add)
                    if n == 1:
                        steps.mark(ins)
            steps.wait()
            steps.mark(v.tensor_tensor(sums[r][:, 0, 1], sums[r][:, 0, 1], euk[:, r, 0], ALU.add))
            steps.mark(v.tensor_tensor(sums[r][:, 1, 1], sums[r][:, 1, 1], euk[:, r, 1], ALU.add))
            steps.wait()
            v.tensor_scalar(sums[r][:, :, 1], sums[r][:, :, 1], DEN_MIN, None, ALU.max).then_inc(s_den, 1)

        def ratio(b, ct, c):
            u, r = b * CT + ct, ct % 2
            dve.wait_ge(s_newton, 2 * u + c + 1)
            if ct == 0 and at_least(b, 2):
                dve.wait_ge(*((s_mm, 12 * (b - 1)) if c == 0 else (s_r2, b - 1)))
            v.scalar_tensor_tensor(out=(r1T, ratio2)[c][:, bass.ds(b % 2, 1), ct, :],
                                   in0=sums[r][:, c, 1].rearrange("p (o t) -> p o t", o=1), scalar=2.0,
                                   in1=sums[r][:, c, 0].rearrange("p (o t) -> p o t", o=1),
                                   op0=ALU.subtract, op1=ALU.mult).then_inc(s_ratio, 1)

        def first_out(b):
            dve.wait_ge(s_sig1, b + 1)
            dve.wait_ge(s_ratio, 2 * CT * (b + 1) - 1)
            r1 = r1T[:, bass.ds(b % 2, 1)].rearrange("p o c t -> p (o c) t")
            v.scalar_tensor_tensor(out=r1, in0=r1, scalar=neg_scale[:, bass.ds(b, 1)], in1=sig[:],
                                   op0=ALU.mult, op1=ALU.mult).then_inc(s_r1, 1)

        def recurrence(b):
            steps = Steps(dve, s_rec_steps, 2 * CT * b)
            for e in range(CT):
                dve.wait_ge(s_gates, CT * b + e + 1)
                steps.do(v.scalar_tensor_tensor(out=z_in[:, e], in0=z_dec[:, e], scalar=1.0, in1=z_in[:, e],
                                                op0=ALU.subtract, op1=ALU.mult))
                steps.do(v.tensor_tensor_scan(z_in[:, e], z_dec[:, e], z_in[:, e], 0.0, ALU.mult, ALU.subtract))
                v.tensor_tensor(z_gate[:, e], z_gate[:, e], z_in[:, e], ALU.mult).then_inc(s_y, 1)

        def residual(b):
            for e in range(CT):
                dve.wait_ge(s_wo, CT * b + e + 1)
                if e == 0:
                    dve.wait_ge(s_y, CT * (b + 1))
                v.scalar_tensor_tensor(out=z_dec[:, e:e + 1], in0=bank(e).rearrange("p (o t) -> p o t", o=1), scalar=vec[:, BOUT, e:e + 1],
                                       in1=xT[:, bass.ds(b % 2, 1), e, :], op0=ALU.add, op1=ALU.add).then_inc(s_x2, 1)

        def second_out(b):
            dve.wait_ge(s_sig2, b + 1)
            v.scalar_tensor_tensor(out=sig[:], in0=ratio2[:, bass.ds(b % 2, 1)].rearrange("p o c t -> p (o c) t"),
                                   scalar=neg_scale[:, bass.ds(b, 1)], in1=sig[:],
                                   op0=ALU.mult, op1=ALU.mult).then_inc(s_r2, 1)

        bc = lambda ap: ap.to_broadcast([P, TT, NE])

        def select(b, st):
            dve.wait_ge(s_logit, b + 1)
            st.do(v.tensor_copy(logit[:], ps_logit))
            dve.nop(nofuse=True)
            for i in range(TT):
                st.mark(v.max(top[:, i], logit[:, i]))
            st.wait()
            v.tensor_tensor(pe_[:], logit[:], bc(top[:, :, 0:1]), ALU.subtract).then_inc(s_shift, 1)
            for i in range(TT):
                st.mark(v.max_index(top_i[:, i], top[:, i], logit[:, i]))
            st.wait()
            st.do(v.tensor_copy(top_f[:], top_i[:]))
            for k in range(TOPK):
                st.mark(v.tensor_tensor(oh[:, k], expert_no[:], bc(top_f[:, :, k:k + 1]), ALU.is_equal))
            st.wait()
            v.tensor_tensor(sel[:], oh[:, 0], oh[:, 1], ALU.add).then_inc(s_sel, 1)
            dve.wait_ge(s_sel, b + 1)
            st.mark(v.tensor_reduce(sel_sum[:], sel[:].rearrange("p i e -> p e i"), AX.X, ALU.add))

        def place(b, st):
            dve.wait_ge(s_init, 16 * NE)
            dve.wait_ge(s_disp, 16 * (1 + TT * TOPK * b))
            st.mark(v.tensor_copy(r2_rows[:, :, C + NE:ROW].bitcast(U32),
                                  token_no[:, bass.ds(b * TT, TT)].rearrange("p (i o) -> p i o", o=1)))
            dve.wait_ge(s_pexp, b + 1)
            st.do(v.tensor_reduce(psum_[:], pe_[:], AX.X, ALU.add))
            st.do(v.reciprocal(psum_[:], psum_[:]))
            st.mark(v.tensor_tensor(r2_rows[:, :, C:C + NE], pe_[:], bc(psum_[:].rearrange("p (i o) -> p i o", o=1)), ALU.mult))
            dve.wait_ge(s_pos, b + 1)
            st.do(v.tensor_scalar(slot_t[:], ps_pos, float(CAP), float(NO_TOKEN), ALU.is_ge, ALU.mult))
            st.do(v.tensor_tensor(slot_f[:], ps_pos, slot_t[:], ALU.add))
            st.do(v.tensor_tensor(slot_f[:], slot_f[:], slot_base[:], ALU.add))
            for k in range(TOPK):
                st.do(v.tensor_tensor(slot_t[:], slot_f[:], oh[:, k], ALU.mult))
                st.do(v.tensor_reduce(dest_f[:, k], slot_t[:], AX.X, ALU.add))
            st.do(v.tensor_tensor(carry[:], carry[:], sel_sum[:], ALU.add))
            dve.wait_ge(s_disp, 16 * (1 + TT * TOPK * b))
            v.tensor_copy(dest[:], dest_f[:]).then_inc(s_dest, 1)
            assert st.n == ROUTE_STEPS, st.n

        dve.wait_ge(s_consts, 2)
        dve.wait_ge(s_pool_setup, 8)
        def step(b, cond, gates, tail):
            st = Steps(dve, s_route, ROUTE_STEPS * (b - 2)) if tail else None
            def gate_operands():
                for n in range(3 * CT):
                    raw, high, low = gate_piece(n)
                    dve.wait_ge(s_gh, n + 1)
                    v.tensor_tensor(low, raw, high.bitcast(F32), ALU.subtract).then_inc(s_gl, 1)

            for s in range(CT):
                if cond:
                    backward(b, s)
                if tail and s == 0:
                    residual(b - 2)
                    if gates and not cond:
                        gate_operands()
                if cond:
                    caps(b if s + 1 < CT else b + 1, (s + 1) % CT)
                    fold(b, s)
                if tail and s == 1:
                    second_out(b - 2)
                if tail and s == 2:
                    select(b - 2, st)
                if cond and s >= 1:
                    ratio(b, s - 1, 0)
                    ratio(b, s - 1, 1)
            if cond:
                ratio(b, CT - 1, 0)
            if gates:
                recurrence(b - 1)
            if cond:
                first_out(b)
                ratio(b, CT - 1, 1)
            if tail:
                place(b - 2, st)

        step(0, True, False, False)
        step(1, True, True, False)
        with dve.Fori(2, B) as b:
            step(b, True, True, True)
        step(B, False, True, True)
        step(B + 1, False, False, True)
        dve.wait_ge(s_count, 1)
        v.tensor_copy(counts[:], ps_count).then_inc(s_count, 1)
        dve.wait_ge(s_count, 2)
        for n, piece in enumerate(pieces(place0)):
            dve.wait_ge(load_sems[3], n + 1)
            weight_low(nc, piece, load_sems[4])


def experts(nc, ctx, ident, counts, rows, place0, load_sems, slots, out_rows, w1, w2):
    def sb(name, shape, dt=F32):
        return ctx.enter_context(nc.sbuf_tensor(name, shape, dt))

    def ps(name, shape, dt=F32):
        return ctx.enter_context(nc.psum_tensor(name, shape, dt))

    def sem(name):
        return ctx.enter_context(nc.semaphore(name))

    place1 = [sb(name, [P, FC, C], F32 if name[0] == "r" else F32R)
              for name in ("raw1_1", "raw2_1", "w1h_1", "w1l_1", "w2h_1", "w2l_1")]
    ring = [place0, place1]
    raw1, raw2, w1h, w1l, w2h, w2l = ([place[n] for place in ring] for n in range(6))
    xh, xl = sb("xh", [P, 2, CT, CAP], F32R), sb("xl", [P, 2, CT, CAP], F32R)
    hh, hl = sb("hh", [P, 2, CAP], F32R), sb("hl", [P, 2, CAP], F32R)
    y = sb("y", [P, ST, C])
    gate = sb("gate", [P, ST])
    token = sb("token", [P, ST], U32)

    ps_y = ps("ps_y", [P, ST, C])
    ps_h = ps("ps_h", [P, 2, 512])
    ps_t = ps("ps_t", [P, CT, P])

    s_w, (s_rows, s_wh, s_wl), s_first_rows = load_sems[:2], load_sems[2:5], load_sems[5:]
    s_tp, s_xh, s_xl = sem("rows_transposed2"), sem("x_high"), sem("x_low")
    s_h, s_hh, s_hl, s_f = sem("hidden_done"), sem("hidden_high"), sem("hidden_low"), sem("hidden_used")
    s_y, s_ya, s_yv = sem("y_done"), sem("y_even"), sem("y_odd")
    s_gate, s_token, s_add = sem("gate_ready"), sem("token_ready"), sem("rows_added")
    s_y0 = sem("y_cleared")

    SPLIT_AT = {0: range(0, 0), 1: range(0, 3), 2: range(3, 7), 3: range(7, 8)}
    TURN_AT = {3: 0, 5: 1, 7: 2, 9: 3, 11: 4}
    HALF = P // 2
    CLASSES = range(4 * HALF, CAP + 1, HALF)

    def by_class(eng, e, body):
        count = eng.value_load(counts[0:1, bass.ds(e, 1)], min_val=0, max_val=B * T)

        def choose(classes):
            if len(classes) == 1:
                body(classes[0])
                return
            middle = (len(classes) - 1) // 2
            with eng.If(count < classes[middle] + 1):
                choose(classes[:middle + 1])
            with eng.Else():
                choose(classes[middle + 1:])
        choose(CLASSES)

    def slot_tiles(n):
        return [(i, min(P, n - i * P)) for i in range(-(-n // P))]

    def hidden_parts(f, n):
        return ((0, 0, n // 2, 1), (1, n // 2, n, 1)) if n > 512 else ((f % 2, 0, n, 2),)

    def turned(e, i):
        return ps_y[:, i, :].rearrange("p (t q) -> p t q", q=P) if isinstance(e, int) else ps_t[:]

    block = ctx.enter_context(nc.Block())

    @block.sync
    def _(sp):
        def weights(e, c):
            load_chunk(sp, s_w, raw1[c % 2][:], raw2[c % 2][:], w1, w2, e, c)

        def expert(e):
            for c in range(NC):
                if not (isinstance(e, int) and c < 2):
                    sp.wait_ge(s_wl, PIECES * (e * NC + (c - 1)))
                if not (isinstance(e, int) and c == 0):
                    weights(e, c)
                if c == 1:
                    sp.wait_ge(s_tp, ST * (e + 1))
                    sp.wait_ge(s_gate, e + 1)
                    sp.wait_ge(s_token, e + 1)
                    load_slot_rows(sp, s_rows, rows, slots, e + 1)

        expert(0)
        with sp.Fori(1, NE) as e:
            expert(e)
        sp.wait_ge(s_wl, PIECES * (NE * NC - 1))
        weights(0, 0)
        sp.wait_ge(s_w[0], 32 * (NE * NC // 2 + 1))
        sp.wait_ge(s_w[1], 32 * (NE * NC // 2))
        sp.wait_ge(s_rows, 16 * (NE + 1))

    @block.gpsimd
    def _(pool):
        nc.gpsimd.memset(y[:], 0.0).then_inc(s_y0, 1)
        def expert(e, first):
            if first:
                for s in s_first_rows:
                    pool.wait_ge(s, 16)
            pool.wait_ge(s_rows, 16 * (e + 1))
            if not first:
                pool.wait_ge(s_add, 16 * ST * e)
            pool.nop(nofuse=True)
            nc.gpsimd.tensor_copy(token[:], rows[:, :, C + NE:ROW].bitcast(U32).rearrange("p i o -> p (i o)")).then_inc(s_token, 1)
            pool.wait_ge(s_token, e + 1)
            pool.wait_ge(s_ya, e + 2)
            pool.wait_ge(s_yv, e + 2)
            pool.wait_ge(s_y0, 1)
            pool.nop(nofuse=True)
            for i in range(ST):
                pool.indirect_dma_start(
                    out=out_rows, out_offset=bass.IndirectOffsetOnAxis(ap=token[:, i:i + 1], axis=0),
                    in_=y[:, i, :], in_offset=None, bounds_check=B * T - 1, oob_is_err=False,
                    compute_op=ALU.add).then_inc(s_add, 16)
        expert(0, True)
        with pool.Fori(1, NE) as e:
            expert(e, False)
        pool.wait_ge(s_add, 16 * ST * NE)

    @block.tensor
    def _(pe):
        def turn(e, i):
            if isinstance(e, int) and i < ST - 1:
                pe.wait_ge(s_first_rows[i], 16)
            else:
                pe.wait_ge(s_rows, 16 * (e + 1))
            if not isinstance(e, int):
                pe.wait_ge(s_xl, ST * e + i)
            for ct in range(CT):
                last = nc.tensor.transpose(turned(e, i)[:, ct, :], rows[:, i, ct * P:(ct + 1) * P], ident[:])
            last.then_inc(s_tp, 1)

        def up(e, par, f, n):
            g = e * NC + f // FC
            if f % FC == 0:
                pe.wait_ge(s_wl, PIECES * (g + 1))
            if f == 0:
                pe.wait_ge(s_xl, ST * (e + 1))
            hidden = e * FT + f
            r, j = (f // FC) % 2, f % FC
            for k, (bank, lo, hi, signals) in enumerate(hidden_parts(f, n)):
                if n > 512:
                    pe.wait_ge(s_hl, 2 * hidden + (k + 1))
                else:
                    pe.wait_ge(s_hl, 2 * hidden + (2 if f == 0 else 0))
                for dt in range(CT):
                    wcol = slice(j * P, (j + 1) * P)
                    o = ps_h[:, bank, 0:hi - lo]
                    nc.tensor.matmul(o, w1h[r][:, dt, wcol], xh[:, par, dt, lo:hi], start=(dt == 0), stop=False)
                    nc.tensor.matmul(o, w1h[r][:, dt, wcol], xl[:, par, dt, lo:hi], start=False, stop=False)
                    last = nc.tensor.matmul(o, w1l[r][:, dt, wcol], xh[:, par, dt, lo:hi], start=False, stop=(dt == CT - 1))
                last.then_inc(s_h, signals)

        def down(e, f, n):
            if f == 0:
                pe.wait_ge(s_ya, e + 1)
                pe.wait_ge(s_yv, e + 1)
            pe.wait_ge(s_hl, 2 * (e * FT + f) + 4)
            r, j = (f // FC) % 2, f % FC
            for i, m in slot_tiles(n):
                tok = slice(i * P, i * P + m)
                nc.tensor.matmul(ps_y[0:m, i, :], hh[:, f % 2, tok], w2h[r][:, j], start=(f == 0), stop=False)
                nc.tensor.matmul(ps_y[0:m, i, :], hl[:, f % 2, tok], w2h[r][:, j], start=False, stop=False)
                last = nc.tensor.matmul(ps_y[0:m, i, :], hh[:, f % 2, tok], w2l[r][:, j], start=False, stop=(f == FT - 1))
            last.then_inc(s_y if f == FT - 1 else s_f, 1)

        for i in range(ST):
            turn(0, i)
        with pe.Fori(0, NE // 2) as pair:
            for par in range(2):
                e = pair * 2 + par

                def body(n):
                    up(e, par, 0, n)
                    for f in range(FT):
                        if f + 1 < FT:
                            up(e, par, f + 1, n)
                        if f in TURN_AT:
                            turn(e + 1, TURN_AT[f])
                        down(e, f, n)
                by_class(pe, e, body)

    @block.scalar
    def _(act):
        a = nc.scalar

        def token_high(e, par, i):
            act.wait_ge(s_tp, ST * e + i + 1)
            a.activation(xh[:, par, :, i * P:(i + 1) * P], turned(e, i), ACT.Copy).then_inc(s_xh, 1)

        act.sem_inc(s_ya, 1)
        for i in range(ST):
            token_high(0, 0, i)
        with act.Fori(0, NE // 2) as pair:
            for par in range(2):
                e = pair * 2 + par

                def body(n):
                    for f in range(FT):
                        hidden = e * FT + f
                        if f >= 2:
                            act.wait_ge(s_f, e * (FT - 1) + (f - 1))
                        for k, (bank, lo, hi, signals) in enumerate(hidden_parts(f, n)):
                            act.wait_ge(s_h, 2 * hidden + (k + signals))
                            a.activation(hh[:, f % 2, lo:hi], ps_h[:, bank, 0:hi - lo], ACT.Relu).then_inc(s_hh, signals)
                        c = f // FC
                        for q in SPLIT_AT[f % FC]:
                            if q == 0 and c > 0:
                                act.wait_ge(s_f, e * (FT - 1) + c * FC)
                            if q == 0:
                                act.wait_ge(s_w[(c + 1) % 2], 32 * (e * (NC // 2) + ((c + 1) // 2 + 1)))
                            weight_high(nc, pieces(ring[(c + 1) % 2])[q], s_wh)
                        if f in TURN_AT:
                            token_high(e + 1, 1 - par, TURN_AT[f])
                    act.wait_ge(s_y, e + 1)
                    act.wait_ge(s_gate, e + 1)
                    act.wait_ge(s_y0, 1)
                    act.wait_ge(s_token, e + 1)
                    for i, m in slot_tiles(n)[0::2]:
                        last = a.activation(y[0:m, i], ps_y[0:m, i, :], ACT.Copy, scale=gate[0:m, i:i + 1])
                    last.then_inc(s_ya, 1)
                by_class(act, e, body)

    @block.vector
    def _(dve):
        v = nc.vector

        def token_low(e, par, i):
            dve.wait_ge(s_xh, ST * e + i + 1)
            s = slice(i * P, (i + 1) * P)
            v.tensor_tensor(xl[:, par, :, s], turned(e, i), xh[:, par, :, s].bitcast(F32), ALU.subtract).then_inc(s_xl, 1)

        dve.sem_inc(s_hl, 2)
        dve.sem_inc(s_yv, 1)
        for s in s_first_rows:
            dve.wait_ge(s, 16)
        for i in range(ST):
            token_low(0, 0, i)
        with dve.Fori(0, NE // 2) as pair:
            for par in range(2):
                e = pair * 2 + par
                dve.wait_ge(s_rows, 16 * (e + 1))
                dve.wait_ge(s_ya, e + 1)
                dve.wait_ge(s_yv, e + 1)
                v.tensor_copy(gate[:], rows[:, :, bass.ds(e + C, 1)].rearrange("p i o -> p (i o)")).then_inc(s_gate, 1)

                def body(n):
                    for f in range(FT):
                        for k, (bank, lo, hi, signals) in enumerate(hidden_parts(f, n)):
                            dve.wait_ge(s_hh, 2 * (e * FT + f) + (k + signals))
                            v.scalar_tensor_tensor(out=hl[:, f % 2, lo:hi], in0=ps_h[:, bank, 0:hi - lo], scalar=0.0,
                                                   in1=hh[:, f % 2, lo:hi].bitcast(F32), op0=ALU.max,
                                                   op1=ALU.subtract).then_inc(s_hl, signals)
                        c = f // FC
                        for q in SPLIT_AT[f % FC]:
                            dve.wait_ge(s_wh, PIECES * (e * NC + (c + 1)) + q + 1)
                            weight_low(nc, pieces(ring[(c + 1) % 2])[q], s_wl)
                        if f in TURN_AT:
                            token_low(e + 1, 1 - par, TURN_AT[f])
                    dve.wait_ge(s_y, e + 1)
                    dve.wait_ge(s_gate, e + 1)
                    dve.wait_ge(s_y0, 1)
                    dve.wait_ge(s_token, e + 1)
                    for i, m in slot_tiles(n)[1::2]:
                        last = v.tensor_scalar(y[0:m, i], ps_y[0:m, i, :], gate[0:m, i:i + 1], None, ALU.mult)
                    last.then_inc(s_yv, 1)
                by_class(dve, e, body)


_INS = ["x", "fside_BxSxS_0", "cond_512", "L0_cond_w", "L0_cond_u", "L0_attn_W_in", "L0_attn_b_in",
        "L0_attn_W_decay", "L0_attn_b_decay", "L0_attn_W_gate", "L0_attn_b_gate", "L0_attn_W_out",
        "L0_attn_b_out", "L0_attn_decay_bias", "L0_cond2_w", "L0_cond2_u", "L0_ffn_Wg", "L0_ffn_w1", "L0_ffn_w2"]


def kernel(**inputs):
    import numpy as _np
    import concourse.bacc as _bacc
    from concourse import mybir as _mybir
    from concourse.bass_utils import run_bass_kernel_spmd as _run

    nc = _bacc.Bacc("TRN2", target_bir_lowering=False, num_devices=1)
    arrays, args = {}, []
    for name in _INS:
        a = _np.ascontiguousarray(inputs[name])
        arrays[f"in_{name}_dram"] = a
        args.append(nc.dram_tensor(f"in_{name}_dram", a.shape, _mybir.dt.from_np(a.dtype), kind="ExternalInput").ap())
    args.append(nc.dram_tensor("out_0_dram", (B, T, C), _mybir.dt.float32, kind="ExternalOutput").ap())
    build_program(nc, *args)
    r = _run(nc, [arrays], core_ids=[0])
    return r.results[0]["out_0_dram"]
```
